# Optimizing a Trainium2 kernel written in Bass

```python
import numpy as np
import jax
import jax.numpy as jnp

def _softmax(x, axis=-1):
    return jax.nn.softmax(x, axis=axis)

def _gelu(x):
    return jax.nn.gelu(x, approximate=True)

def _silu(x):
    return jax.nn.silu(x)

def _sigmoid(x):
    return jax.nn.sigmoid(x)

def _layernorm(x, axis=-1, eps=1e-05):
    m = jnp.mean(x, axis=axis, keepdims=True)
    v = jnp.var(x, axis=axis, keepdims=True)
    return (x - m) / jnp.sqrt(v + eps)

def _scatter_add(tgt, idx, src, axis=0):
    return tgt.at[idx].add(src)

def _segment_sum(src, seg, n):
    return jax.ops.segment_sum(src, seg, n)
kernel_name = 'mk_adj_preln_d1_adj_r2_b0ef6a'

def setup_inputs(seed: int=0):
    np.random.seed(seed)
    _w = jnp.asarray

    def _rec_inputs():
        import jax
        import jax.numpy as jnp
        _gk = jax.random.key(seed)
        x = 7.22e-05 + 1 * jax.random.normal(jax.random.fold_in(_gk, 1), (8, 1024, 512), jnp.float32)
        _a = jax.random.bernoulli(jax.random.fold_in(_gk, 2), 0.0078125, (8, 1024, 1024))
        _a = jnp.logical_or(_a, jnp.swapaxes(_a, -1, -2))
        _a = jnp.logical_or(_a, jnp.eye(1024, dtype=bool))
        _af = _a.astype(jnp.float32)
        _af = _af * jax.random.uniform(jax.random.fold_in(_gk, 3), (8, 1024, 1024), jnp.float32, 0.05, 4.42607)
        adj = _af
        return (x, adj)
    x, adj = _rec_inputs()

    def _L0_gnn_setup():
        import jax, jax.numpy as jnp
        import numpy as np
        NUM_HEADS = 16
        key = jax.random.key(seed)
        ks = jax.random.split(key, 7)
        B, N, D = (16, 256, 512)
        return {'x': jax.random.normal(ks[0], (B, N, D), dtype=jnp.float32), 'spatial_encoding': jax.random.normal(ks[1], (B, N, N), dtype=jnp.float32), 'edge_encoding': jax.random.normal(ks[2], (B, N, N), dtype=jnp.float32), 'Wq': jax.random.normal(ks[3], (D, D), dtype=jnp.float32) * D ** (-0.5), 'Wk': jax.random.normal(ks[4], (D, D), dtype=jnp.float32) * D ** (-0.5), 'Wv': jax.random.normal(ks[5], (D, D), dtype=jnp.float32) * D ** (-0.5), 'Wo': jax.random.normal(ks[6], (D, D), dtype=jnp.float32) * D ** (-0.5)}
    _L0_gnn_all = _L0_gnn_setup()
    _L0_gnn_in = {k: v for k, v in _L0_gnn_all.items() if k in ('Wq', 'Wk', 'Wv', 'Wo')}
    del _L0_gnn_all
    return {'x': x, 'adj': adj, 'L0_gnn_Wq': _L0_gnn_in['Wq'], 'L0_gnn_Wk': _L0_gnn_in['Wk'], 'L0_gnn_Wv': _L0_gnn_in['Wv'], 'L0_gnn_Wo': _L0_gnn_in['Wo']}

def reference(x, adj, L0_gnn_Wq, L0_gnn_Wk, L0_gnn_Wv, L0_gnn_Wo):
    import jax
    import jax.numpy as jnp

    def _L0_gnn_ref(x, spatial_encoding, edge_encoding, Wq, Wk, Wv, Wo):
        import jax, jax.numpy as jnp
        import numpy as np
        NUM_HEADS = 16
        B, N, D = x.shape
        H = NUM_HEADS
        hd = D // H
        scale = D ** (-0.5)

        def split_heads(t):
            return t.reshape(B, N, H, hd).transpose(0, 2, 1, 3)
        q = split_heads(x @ Wq.T)
        k = split_heads(x @ Wk.T)
        v = split_heads(x @ Wv.T)
        bias = (spatial_encoding + edge_encoding)[:, None]
        a = jnp.einsum('bhnd,bhmd->bhnm', q, k) * scale + bias
        row_nonzero = jnp.any(a != 0, axis=-1, keepdims=True)
        a = jnp.where(row_nonzero, a, -jnp.inf)
        p = jax.nn.softmax(a, axis=-1)
        p = jnp.where(jnp.isnan(p), 0.0, p)
        o = jnp.einsum('bhnm,bhmd->bhnd', p, v)
        o = o.transpose(0, 2, 1, 3).reshape(B, N, D)
        return o @ Wo.T
    h = jnp.maximum(_layernorm(x, axis=-1), 0.0)
    x = x + _L0_gnn_ref(h, adj, adj, L0_gnn_Wq, L0_gnn_Wk, L0_gnn_Wv, L0_gnn_Wo)
    return x

_drawn_inputs = setup_inputs


def setup_inputs(seed=0):
    import zlib

    import numpy as np

    out = dict(_drawn_inputs(seed))
    spreads = {}
    factors = {'L0_gnn_Wq': 3.005, 'L0_gnn_Wk': 2.957}
    for name, (base, spread) in spreads.items():
        noise = np.random.default_rng([zlib.crc32(name.encode()), seed]).standard_normal(out[name].shape)
        drawn = base * np.exp(spread * noise) if base else spread * noise
        out[name] = jnp.asarray(drawn.astype(out[name].dtype))
    for name, factor in factors.items():
        out[name] = (out[name] * factor).astype(out[name].dtype)
    return out
```

```python
from contextlib import ExitStack

import concourse.bass as bass
from concourse import mybir

F32 = mybir.dt.float32
F32R = mybir.dt.float32r
ALU = mybir.AluOpType
ACT = mybir.ActivationFunctionType

P = 128
B, N, D = 8, 1024, 512
H = 16
HD = D // H
J = P // HD
G = H // J
T = N // P
KC = D // P
SLOTS = T * 8
BSLOTS = G * SLOTS
STEPS = G * T * J
EPS = 1e-5
SCALE = D ** -0.5
BIG = 3.0e38

T_LAG = 10
PV_LAG = 12
DVE_BLOCKS = (0, 3, 6)
TAIL = PV_LAG + 5


def plan():
    parts = []
    for g in range(G):
        base = g * SLOTS
        late, early = 13, 45
        if g == 0:
            where = {("k", 0): (0, 1, 2, 3), ("k", 1): (4, 5, 6, 7), ("q", 0): (9, 10, 11, 12),
                     ("q", 1): (50, 51, 52, 53), ("v", 0): (54, 55, 56, 57), ("v", 1): (58, 59, 60, 61)}
            for t in range(T):
                where["o", t] = tuple(18 + int(0.84 * (4 * t + p)) for p in range(4))
        elif g == G - 1:
            where = {("k", 0): (18, 19, 20, 21), ("k", 1): (23, 24, 25, 26), ("q", 0): (28, 29, 30, 31),
                     ("q", 1): (33, 34, 35, 36), ("v", 0): (39, 40, 41, 42), ("v", 1): (50, 51, 52, 53)}
            for t in range(T // 2, T):
                where["hT", t] = ((8, 9, 10, 12)[t - T // 2],)
        else:
            where = {("k", 0): (0, 2, 4, 6), ("k", 1): (7, 9, 11, 12), ("q", 0): (18, 20, 22, 24),
                     ("q", 1): (26, 28, 30, 32), ("v", 0): (35, 37, 39, 41), ("v", 1): (50, 52, 54, 56)}
        where["rT", 1], where["rB", 1] = (late,), (late + 3,)
        where["rT", 0], where["rB", 0] = (early,), (early + 3,)
        if g == G - 2:
            for t in range(T // 2):
                where["hT", t] = (58 + t,)
        for unit, slots in sorted(where.items(), key=lambda kv: kv[1][0]):
            for p, s in enumerate(slots):
                parts.append((base + s, g, unit, p, p == len(slots) - 1))
    return parts


PLAN = plan()


def exists(g, unit, first, last):
    if first and g == 0 and (unit[0] == "o" or unit in (("rT", 1), ("rB", 1))):
        return False
    return not (last and (unit[0] == "hT" or (g == G - 1 and unit[0] in ("k", "q", "v"))))


def ranks(first, last):
    order = [(g, u) for _, g, u, p, _ in PLAN if p == 0 and exists(g, u, first, last)]
    return {x: n for n, x in enumerate(order)}


RANK = {(f, la): ranks(f, la) for f in (False, True) for la in (False, True)}
UNITS = len(RANK[False, False])
FIRST_UNITS = len(RANK[True, False])
HEAD_UNITS = T + 6
LACK = UNITS - FIRST_UNITS


def adj_gnn(nc, x, adj, wq, wk, wv, wo, ident_in, pick_in, out):
    with ExitStack() as ctx:
        def sb(name, shape, dt=F32):
            return ctx.enter_context(nc.sbuf_tensor(name, shape, dt))

        def psum(name, shape):
            return ctx.enter_context(nc.psum_tensor(name, shape, F32))

        def sem(name):
            return ctx.enter_context(nc.semaphore(name))

        ident = sb("ident", [P, P])
        pick = sb("pick", [J * 4, 4, P])
        half = sb("half", [P, 1])
        w_chunk = {n: sb(f"w{n}_chunk", [P, KC, P]) for n in "qkv"}
        wo_sb = sb("wo_sb", [P, KC, D])
        xbuf = sb("xbuf", [P, 4, D])
        stats = sb("stats", [P, 4, 6])
        moments = sb("moments", [P, 4, 2])
        rstd = sb("rstd", [P, 4])
        var_eps = sb("var_eps", [P, 4])
        hT = sb("hT", [P, KC, N])
        k_hi = sb("k_hi", [P, N], F32R)
        k_lo = sb("k_lo", [P, N], F32R)
        q_hi = sb("q_hi", [P, N], F32R)
        q_lo = sb("q_lo", [P, N], F32R)
        k_stack = sb("k_stack", [P, 2, J, N], F32R)
        q_stack = sb("q_stack", [P, J, N], F32R)
        v_sb = sb("v_sb", [P, 2, T, P])
        adj_sb = sb("adj_sb", [P, T, N])
        probs = sb("probs", [P, 2, J, N])
        probsT = sb("probsT", [P, 4, J * P])
        neg_max = sb("neg_max", [P, 2, T * J])
        row_sum = sb("row_sum", [P, 2, T * J])
        inv = sb("inv", [P, 16])
        nonzero = sb("nonzero", [P, 16])
        keep = sb("keep", [P, 16])
        rinv = sb("rinv", [P, 16])
        rT = sb("rT", [16, P])
        o_raw = sb("o_raw", [P, D])
        oT = sb("oT", [P, G, N])

        scores = psum("scores", [P, 2, N])
        blockT = psum("blockT", [P, 2, J * P])
        o_acc = psum("o_acc", [P, D])
        side = psum("side", [P, D])

        const_loaded = sem("const_loaded")
        half_set = sem("half_set")
        passed = sem("passed")
        wo_loaded = sem("wo_loaded")
        w_loaded = {n: sem(f"w{n}_loaded") for n in "qkv"}
        adj_loaded = [sem(f"adj_loaded{t}") for t in range(T)]
        x_loaded = [sem(f"x_loaded{i}") for i in range(4)]
        stats_done = sem("stats_done")
        moments_done = sem("moments_done")
        eps_added = sem("eps_added")
        rstd_done = sem("rstd_done")
        normed = sem("normed")
        side_computed = sem("side_computed")
        hi_split = sem("hi_split")
        side_retired = sem("side_retired")
        k_stacked = [sem(f"k_stacked{c}") for c in range(2)]
        q_stacked = [sem(f"q_stacked{c}") for c in range(2)]
        qk_done = sem("qk_done")
        max_done = sem("max_done")
        exp_done = sem("exp_done")
        block_done = sem("block_done")
        act_brought = sem("act_brought")
        dve_brought = sem("dve_brought")
        pv_done = sem("pv_done")
        o_brought = sem("o_brought")
        r_step = sem("r_step")
        r_ready = sem("r_ready")
        y_stored = [sem(f"y_stored{i}") for i in range(4)]

        block = ctx.enter_context(nc.Block())

        def wait(eng, s, value):
            if not isinstance(value, int) or value > 0:
                eng.wait_ge(s, value)

        def wait_apart(eng, s, value):
            wait(eng, s, value)
            if not isinstance(value, int):
                eng.sem_inc(passed, 1)

        def unit_index(b, first, last, g, unit):
            r = RANK[first, last][g, unit]
            if first:
                return HEAD_UNITS + r
            return b * UNITS + (HEAD_UNITS - LACK) + r

        def end_index(n):
            return (B - 1) * UNITS + (HEAD_UNITS - LACK) + len(RANK[False, True]) + n

        def brought(eng, i_tile, mi):
            if mi in DVE_BLOCKS:
                wait(eng, dve_brought, i_tile * len(DVE_BLOCKS) + DVE_BLOCKS.index(mi) + 1)
            else:
                acts = [m for m in range(8) if m not in DVE_BLOCKS]
                wait(eng, act_brought, i_tile * len(acts) + acts.index(mi) + 1)

        def bodies(eng, body, tail):
            body(0, True, False)
            with eng.Fori(1, B - 1) as b:
                body(b, False, False)
            body(B - 1, False, True)
            tail()

        def units_ending(kap, first, last):
            return [(g, u) for s, g, u, _, end in PLAN if s == kap and end and exists(g, u, first, last)]

        @block.sync
        def _(sp):
            sp.dma_start(ident[:, :], ident_in).then_inc(const_loaded, 16)
            sp.dma_start(pick[:, :, :], pick_in).then_inc(const_loaded, 16)

            def load_x(b, t, after_norm):
                if after_norm:
                    if t >= 4:
                        wait_apart(sp, y_stored[t % 4], (b * 2 + 1) * 16)
                sp.dma_start(xbuf[:, t % 4, :], x[b, t * P:(t + 1) * P, :]).then_inc(x_loaded[t % 4], 16)

            def load_w(n, g):
                w = {"q": wq, "k": wk, "v": wv}[n]
                sp.dma_start(w_chunk[n][:, :, :],
                             w.rearrange("(c p) o -> p c o", p=P)[:, :, g * P:(g + 1) * P]).then_inc(w_loaded[n], 16)

            def stack_k(buf, c, index):
                wait_apart(sp, side_retired, index + 1)
                for j in range(J):
                    for quad, part in enumerate((k_hi, k_lo, k_hi, k_lo)):
                        sp.dma_start(k_stack[quad * HD:(quad + 1) * HD, buf, j, c * D:(c + 1) * D].bitcast(F32),
                                     part[j * HD:(j + 1) * HD, c * D:(c + 1) * D].bitcast(F32)).then_inc(k_stacked[c], 16)

            def stack_q(c, index, used):
                wait_apart(sp, side_retired, index + 1)
                wait_apart(sp, qk_done, used)
                cols = slice(c * D, (c + 1) * D)
                for j in range(J):
                    for quad, part in enumerate((q_hi, q_hi, q_lo, q_lo)):
                        sp.dma_start(q_stack[quad * HD:(quad + 1) * HD, j, cols].bitcast(F32),
                                     part[j * HD:(j + 1) * HD, cols].bitcast(F32)).then_inc(q_stacked[c], 16)

            def store_y(b, t, index):
                wait_apart(sp, side_retired, index + 1)
                sp.dma_start(out[b, t * P:(t + 1) * P, :], xbuf[:, t % 4, :]).then_inc(y_stored[t % 4], 16)

            for t in range(4):
                load_x(0, t, False)
            for n in "kqv":
                load_w(n, 0)
            for t in range(4, T):
                wait_apart(sp, side_computed, t - 3)
                load_x(0, t, False)
            for t in range(T):
                sp.dma_start(adj_sb[:, t, :], adj[0, t * P:(t + 1) * P, :]).then_inc(adj_loaded[t], 16)
            for c in range(2):
                stack_k(0, c, T + c)
            for c in range(2):
                stack_q(c, T + 2 + c, 0)
            sp.dma_start(wo_sb[:, :, :], wo.rearrange("(c p) o -> p c o", p=P)).then_inc(wo_loaded, 16)
            wait_apart(sp, side_computed, HEAD_UNITS)
            for n in "kqv":
                load_w(n, 1)

            def body(b, first, last):
                for kap in range(BSLOTS):
                    g, lam = kap // SLOTS, kap % SLOTS
                    for gu, u in units_ending(kap - 1, first, last):
                        index = unit_index(b, first, last, gu, u)
                        if u[0] == "k":
                            stack_k((gu + 1) % 2, u[1], index)
                        if u in (("k", 1), ("q", 1), ("v", 1)) and not (last and gu == G - 2):
                            wait_apart(sp, side_computed, index + 1)
                            load_w(u[0], (gu + 2) % G)
                        if u[0] == "o":
                            store_y(b - 1, u[1], index)
                            if u[1] < 4:
                                load_x(b - 1, u[1] + 4, True)
                        if u[0] == "hT" and u[1] < 4:
                            wait_apart(sp, side_computed, index + 1)
                            load_x(b + 1, u[1] + 4, False)
                    if not (last and g == G - 1):
                        for c in range(2):
                            ready = [s + 1 for s, gu, u, _, end in PLAN
                                     if gu == g and u == ("q", c) and end][0] - g * SLOTS
                            if lam == max(ready, c * 32 + 31):
                                index = unit_index(b, first, last, g, ("q", c))
                                stack_q(c, index, b * STEPS + (g * T + 4 * c + 4) * J)
                    if g == G - 1 and not last and lam % 8 == 7:
                        t = lam // 8
                        wait_apart(sp, max_done, b * STEPS + (g * T + t) * J + J)
                        sp.dma_start(adj_sb[:, t, :], adj[b + 1, t * P:(t + 1) * P, :]).then_inc(adj_loaded[t], 16)
                    if g == 1 and lam in (10, 12, 14, 16) and not last:
                        t = (lam - 10) // 2
                        if not first:
                            wait_apart(sp, y_stored[t], b * 2 * 16)
                        load_x(b + 1, t, False)
                    if g == G - 1 and lam in (52, 54, 56, 58):
                        t = (lam - 52) // 2
                        if last:
                            wait_apart(sp, y_stored[t], b * 2 * 16)
                        else:
                            wait_apart(sp, side_computed, unit_index(b, first, last, g, ("hT", t + 4)) + 1)
                        load_x(b, t, True)

            def tail():
                for t in range(T):
                    store_y(B - 1, t, end_index(2 + t))
                    if t < 4:
                        load_x(B - 1, t + 4, True)
                for i in range(4):
                    wait_apart(sp, y_stored[i], B * 2 * 16)

            bodies(sp, body, tail)

        @block.tensor
        def _(pe):
            def side_part(b, g, unit, p, end, index):
                kind, c = unit
                if p == 0:
                    wait(pe, side_retired, index)
                if kind == "hT":
                    wait(pe, normed, b * T + c + 1)
                    for i in range(KC):
                        last = nc.tensor.transpose(side[:, i * P:(i + 1) * P],
                                                   xbuf[:, c % 4, i * P:(i + 1) * P], ident[:, :])
                elif kind in "kq":
                    if p == 0:
                        wait(pe, w_loaded[kind], (b * G + g + 1) * 16)
                    last = nc.tensor.matmul(side[:, :], w_chunk[kind][:, p, :], hT[:, p, c * D:(c + 1) * D],
                                            start=p == 0, stop=p == KC - 1)
                elif kind == "v":
                    if p == 0:
                        wait(pe, w_loaded["v"], (b * G + g + 1) * 16)
                    for i in range(KC):
                        rows = slice((c * 4 + p) * P, (c * 4 + p + 1) * P)
                        last = nc.tensor.matmul(side[:, p * P:(p + 1) * P], hT[:, i, rows], w_chunk["v"][:, i, :],
                                                start=i == 0, stop=i == KC - 1)
                elif kind == "rT":
                    wait(pe, r_ready, b * G * 2 + g * 2 + c + 1)
                    last = nc.tensor.transpose(side[0:16, 0:P], rinv[:, :], ident[:, :])
                elif kind == "rB":
                    for i in range(4):
                        last = nc.tensor.matmul(side[:, i * P:(i + 1) * P], pick[:, i, :], rT[:, :],
                                                start=True, stop=True)
                elif kind == "o":
                    last = nc.tensor.matmul(side[:, :], oT[:, p, c * P:(c + 1) * P], wo_sb[:, p, :],
                                            start=p == 0, stop=p == KC - 1)
                if end:
                    last.then_inc(side_computed, 1)

            def transposes(tile, t, mi):
                if mi == 0:
                    wait(pe, exp_done, tile * J + J)
                if mi >= 2:
                    brought(pe, tile, mi - 2)
                else:
                    brought(pe, tile - 1, mi + 6)
                for j in range(J):
                    last = nc.tensor.transpose(blockT[:, mi % 2, j * P:(j + 1) * P],
                                               probs[:, t % 2, j, mi * P:(mi + 1) * P], ident[:, :])
                last.then_inc(block_done, 1)

            def products(tile, half_index, gi, t, mi):
                brought(pe, tile, mi)
                if mi == 0 and t % 4 == 0:
                    wait(pe, o_brought, half_index)
                for j in range(J):
                    last = nc.tensor.matmul(o_acc[j * HD:(j + 1) * HD, (t % 4) * P:(t % 4 + 1) * P],
                                            v_sb[:, gi % 2, mi, j * HD:(j + 1) * HD],
                                            probsT[:, mi % 4, j * P:(j + 1) * P],
                                            start=mi == 0, stop=mi == 7, tile_position=(0, j * HD))
                last.then_inc(pv_done, 1)

            wait(pe, const_loaded, 32)
            for t in range(T):
                side_part(0, 0, ("hT", t), 0, True, t)
            for n, unit in enumerate([("k", 0), ("k", 1), ("q", 0), ("q", 1), ("v", 0), ("v", 1)]):
                for p in range(4):
                    side_part(0, 0, unit, p, p == 3, T + n)

            def body(b, first, last):
                for kap in range(BSLOTS + (TAIL if last else 0)):
                    g, t, mi = kap // SLOTS, kap % SLOTS // 8, kap % 8
                    if kap < BSLOTS and mi % 2 == 0:
                        j = mi // 2
                        s = kap // 2
                        if t % 4 == 0 and j == 0:
                            wait(pe, q_stacked[t // 4], (b * G + g + 1) * 16 * J * 4)
                        if t == 0 and j == 0:
                            for c in range(2):
                                wait(pe, k_stacked[c], (b * G + g + 1) * 16 * J * 4)
                        wait(pe, exp_done, b * STEPS + s - 1)
                        for c in range(2):
                            mm = nc.tensor.matmul(scores[:, s % 2, c * D:(c + 1) * D],
                                                  q_stack[:, j, t * P:(t + 1) * P],
                                                  k_stack[:, g % 2, j, c * D:(c + 1) * D], start=True, stop=True)
                        mm.then_inc(qk_done, 1)
                    i = kap - T_LAG
                    if not (first and i < 0) and i < BSLOTS:
                        transposes(b * G * T + i // 8, i // 8 % T, i % 8)
                    for s, gu, u, p, end in PLAN:
                        if s != kap or not exists(gu, u, first, last):
                            continue
                        if u[0] == "hT":
                            bb, gg = b + 1, 0
                        elif u[0] in "kqv":
                            bb, gg = (b, gu + 1) if gu + 1 < G else (b + 1, 0)
                        elif u in (("rT", 1), ("rB", 1)):
                            bb, gg = b, gu - 1
                        else:
                            bb, gg = b, gu
                        side_part(bb, gg, u, p, end, unit_index(b, first, last, gu, u))
                    if kap % 2 == PV_LAG % 2:
                        continue
                    for i in (kap - PV_LAG - 1, kap - PV_LAG):
                        if not (first and i < 0) and i < BSLOTS:
                            products(b * G * T + i // 8, b * G * 2 + i // 32, i // SLOTS % G, i // 8 % T, i % 8)

            def tail():
                for n, unit in enumerate([("rT", 1), ("rB", 1)] + [("o", t) for t in range(T)]):
                    for p in range(4 if unit[0] == "o" else 1):
                        side_part(B - 1, G - 1, unit, p, unit[0] != "o" or p == 3, end_index(n))

            wait(pe, wo_loaded, 16)
            bodies(pe, body, tail)

        @block.scalar
        def _(act):
            def retire(b, g, unit, index):
                kind, c = unit
                if kind == "hT":
                    act.wait_ge(side_computed, index + 1)
                    nc.scalar.activation(hT[:, :, c * P:(c + 1) * P],
                                         side[:, :].rearrange("p (i n) -> p i n", i=KC), ACT.Relu
                                         ).then_inc(side_retired, 1)
                elif kind == "v":
                    act.wait_ge(side_computed, index + 1)
                    nc.scalar.activation(v_sb[:, g % 2, c * 4:(c + 1) * 4, :],
                                         side[:, :].rearrange("p (i n) -> p i n", i=4), ACT.Copy
                                         ).then_inc(side_retired, 1)
                elif kind == "k":
                    act.wait_ge(side_computed, index + 1)
                    wait(act, k_stacked[c], (b * G + g) * 16 * J * 4)
                    nc.scalar.activation(k_hi[:, c * D:(c + 1) * D], side[:, :], ACT.Copy).then_inc(hi_split, 1)
                elif kind == "q":
                    act.wait_ge(side_computed, index + 1)
                    wait(act, q_stacked[c], (b * G + g) * 16 * J * 4)
                    nc.scalar.activation(q_hi[:, c * D:(c + 1) * D], side[:, :], ACT.Copy, scale=SCALE / 2
                                         ).then_inc(hi_split, 1)

            def bring(tile, mi):
                act.wait_ge(block_done, tile * 8 + mi + 1)
                wait(act, pv_done, tile * 8 + mi - 3)
                nc.scalar.activation(probsT[:, mi % 4, :], blockT[:, mi % 2, :], ACT.Copy).then_inc(act_brought, 1)

            def bring_o(half_index, pv_count, rb_retired):
                act.wait_ge(pv_done, pv_count)
                wait(act, side_retired, rb_retired)
                nc.scalar.activation(o_raw[:, :], o_acc[:, :], ACT.Copy).then_inc(o_brought, 1)

            for t in range(T):
                retire(0, 0, ("hT", t), t)
            for n, unit in enumerate([("k", 0), ("k", 1), ("q", 0), ("q", 1), ("v", 0), ("v", 1)]):
                retire(0, 0, unit, T + n)

            def body(b, first, last):
                for kap in range(BSLOTS + (TAIL if last else 0)):
                    g, t, mi = kap // SLOTS, kap % SLOTS // 8, kap % 8
                    i = kap - T_LAG
                    if i % 8 not in DVE_BLOCKS and not (first and i < 0) and i < BSLOTS:
                        bring(b * G * T + i // 8, i % 8)
                    if kap < BSLOTS and mi % 2 == 1:
                        j, s = mi // 2, kap // 2
                        act.wait_ge(max_done, b * STEPS + s + 1)
                        if j == 0:
                            wait(act, block_done, (b * G * T + g * T + t - 1) * 8)
                        nc.scalar.activation(probs[:, t % 2, j, :], scores[:, s % 2, :], ACT.Exp,
                                             bias=neg_max[:, g % 2, t * J + j:t * J + j + 1], scale=-1.0,
                                             accum_out=row_sum[:, g % 2, t * J + j:t * J + j + 1]
                                             ).then_inc(exp_done, 1)
                    i = kap - PV_LAG
                    if i % 32 == 31 and not (first and i < 0) and i < BSLOTS:
                        hh = i // 32
                        if first and hh == 0:
                            before = 0
                        elif hh < 0:
                            before = b * UNITS + (HEAD_UNITS - LACK) - (UNITS - RANK[False, False][G - 1, ("rB", 0)]) + 1
                        elif hh % 2 == 0:
                            before = unit_index(b, first, last, hh // 2, ("rB", 1)) + 1
                        else:
                            before = unit_index(b, first, last, hh // 2, ("rB", 0)) + 1
                        bring_o(hh, (b * BSLOTS) + i + 1, before)
                    for gu, u in units_ending(kap, first, last):
                        bb, gg = (b, gu)
                        if u[0] in "kqv":
                            bb, gg = (b, gu + 1) if gu + 1 < G else (b + 1, 0)
                        retire(bb, gg, u, unit_index(b, first, last, gu, u))

            bodies(act, body, lambda: None)

        @block.vector
        def _(dve):
            def norm_stats(b, t):
                slot = t % 4
                dve.wait_ge(x_loaded[slot], norm_loads(b, t))
                nc.vector.bn_stats(stats[:, slot, :], xbuf[:, slot, :]).then_inc(stats_done, 1)
                wait_apart(dve, stats_done, b * T + t + 1)
                nc.vector.bn_aggr(moments[:, slot, :], stats[:, slot, :]).then_inc(moments_done, 1)

            def norm_loads(b, t):
                before = 0 if isinstance(b, int) and b == 0 else 4 * b - 2
                return (before + t // 4 + 1) * 16

            def normalise(b, t):
                slot = t % 4
                dve.wait_ge(rstd_done, b * T + t + 1)
                nc.vector.tensor_scalar(xbuf[:, slot, :], xbuf[:, slot, :], moments[:, slot, 0:1],
                                        rstd[:, slot:slot + 1], ALU.subtract, ALU.mult).then_inc(normed, 1)

            def retire(b, g, unit, index):
                kind, c = unit
                if kind in "kq" and len(kind) == 1:
                    dve.wait_ge(hi_split, split_count(b, g, kind, c))
                    hi, lo = (x[:, c * D:(c + 1) * D] for x in ((k_hi, k_lo) if kind == "k" else (q_hi, q_lo)))
                    nc.vector.scalar_tensor_tensor(lo, side[:, :], 1.0 if kind == "k" else SCALE / 2,
                                                   hi.bitcast(F32), ALU.mult, ALU.subtract).then_inc(side_retired, 1)
                elif kind == "rT":
                    dve.wait_ge(side_computed, index + 1)
                    nc.vector.tensor_copy(rT[:, :], side[0:16, 0:P]).then_inc(side_retired, 1)
                elif kind == "rB":
                    dve.wait_ge(side_computed, index + 1)
                    dve.wait_ge(o_brought, (b * G + g) * 2 + c + 1)
                    nc.vector.tensor_tensor(oT[:, g % G, c * D:(c + 1) * D], side[:, :], o_raw[:, :],
                                            ALU.mult).then_inc(side_retired, 1)
                elif kind == "o":
                    dve.wait_ge(side_computed, index + 1)
                    dve.wait_ge(x_loaded[c % 4], sum_loads(b, c))
                    nc.vector.tensor_tensor(xbuf[:, c % 4, :], side[:, :], xbuf[:, c % 4, :],
                                            ALU.add).then_inc(side_retired, 1)

            def split_count(b, g, kind, c):
                return (b * G + g) * 4 + (0 if kind == "k" else 2) + c + 1

            def sum_loads(b, t):
                if isinstance(b, int) and b == B - 1:
                    return (b * 4 + 2 + t // 4 + 1) * 16
                return (b * 4 + 4 + t // 4 + 1) * 16

            def invert(b, g, c, transposed):
                half_index = (b * G + g) * 2 + c
                cols = slice(16 * c, 16 * c + 16)
                dve.wait_ge(exp_done, (b * G + g) * T * J + 16 * (c + 1))
                wait(dve, side_computed, transposed)
                nc.vector.reciprocal(inv[:, :], row_sum[:, g % 2, cols]).then_inc(r_step, 1)
                nc.vector.tensor_scalar(nonzero[:, :], neg_max[:, g % 2, cols], 0.0, None,
                                        ALU.not_equal).then_inc(r_step, 1)
                dve.wait_ge(r_step, half_index * 3 + 2)
                nc.vector.scalar_tensor_tensor(keep[:, :], row_sum[:, g % 2, cols], float(N), nonzero[:, :],
                                               ALU.is_lt, ALU.max).then_inc(r_step, 1)
                dve.wait_ge(r_step, half_index * 3 + 3)
                nc.vector.tensor_tensor(rinv[:, :], inv[:, :], keep[:, :], ALU.mult).then_inc(r_ready, 1)

            nc.vector.memset(half[:, :], -0.5).then_inc(half_set, 1)
            for t in range(T + 2):
                if t < T:
                    norm_stats(0, t)
                if t >= 1 and t - 1 < T:
                    normalise(0, t - 1)
            for n, unit in enumerate([("k", 0), ("k", 1), ("q", 0), ("q", 1)]):
                retire(0, 0, unit, T + n)

            def body(b, first, last):
                for kap in range(BSLOTS + (TAIL if last else 0)):
                    g, t, mi = kap // SLOTS, kap % SLOTS // 8, kap % 8
                    lam = kap % SLOTS
                    if kap < BSLOTS and mi % 2 == 0:
                        j, s = mi // 2, kap // 2
                        wait_apart(dve, qk_done, b * STEPS + s + 1)
                        if g == 0 and j == 0:
                            wait_apart(dve, adj_loaded[t], (b + 1) * 16)
                        nc.vector.tensor_tensor_reduce(
                            out=scores[:, s % 2, :], in0=scores[:, s % 2, :], in1=adj_sb[:, t, :], scale=-2.0,
                            scalar=BIG, op0=ALU.add, op1=ALU.min,
                            accum_out=neg_max[:, g % 2, t * J + j:t * J + j + 1]).then_inc(max_done, 1)
                    i = kap - T_LAG
                    if i % 8 in DVE_BLOCKS and not (first and i < 0) and i < BSLOTS:
                        tile, m = b * G * T + i // 8, i % 8
                        dve.wait_ge(block_done, tile * 8 + m + 1)
                        wait(dve, pv_done, tile * 8 + m - 3)
                        nc.vector.tensor_copy(probsT[:, m % 4, :], blockT[:, m % 2, :]).then_inc(dve_brought, 1)
                    for s, gu, u, _, _ in PLAN:
                        if u[0] == "rT" and s - 2 == kap and exists(gu, u, first, last):
                            gg = gu - 1 if u[1] == 1 else gu
                            invert(b, gg, u[1], rt_last(b, first, last, gu, u))
                    if last and kap == BSLOTS + 11:
                        invert(b, G - 1, 1, unit_index(b, first, last, G - 1, ("rT", 0)) + 1)
                    if not last:
                        for t2 in range(T):
                            hs = [s for s, gu, u, _, _ in PLAN if u == ("hT", t2)][0]
                            if hs - 7 == kap:
                                norm_stats(b + 1, t2)
                            if hs - 3 == kap:
                                normalise(b + 1, t2)
                    for gu, u in units_ending(kap, first, last):
                        bb, gg = (b, gu)
                        if u[0] in "kqv":
                            bb, gg = (b, gu + 1) if gu + 1 < G else (b + 1, 0)
                        elif u[0] == "rB" and u[1] == 1:
                            bb, gg = (b, gu - 1) if gu > 0 else (b - 1, G - 1)
                        elif u[0] == "o":
                            bb = b - 1
                        retire(bb, gg, u, unit_index(b, first, last, gu, u))

            def rt_last(b, first, last, gu, u):
                if u == ("rT", 0):
                    if first and gu == 0:
                        return 0
                    return unit_index(b, first, last, gu, ("rT", 1)) + 1
                if gu > 0:
                    return unit_index(b, first, last, gu - 1, ("rT", 0)) + 1
                return b * UNITS + (HEAD_UNITS - LACK) - (UNITS - RANK[False, False][G - 1, ("rT", 0)]) + 1

            def tail():
                retire(B - 1, G - 1, ("rT", 1), end_index(0))
                retire(B - 1, G - 1, ("rB", 1), end_index(1))
                for t in range(T):
                    retire(B - 1, G - 1, ("o", t), end_index(2 + t))

            bodies(dve, body, tail)

        @block.gpsimd
        def _(pool):
            pool.wait_ge(half_set, 1)
            with pool.Fori(0, B) as b:
                for t in range(T):
                    slot = t % 4
                    wait_apart(pool, moments_done, b * T + t + 1)
                    nc.gpsimd.tensor_scalar(var_eps[:, slot:slot + 1], moments[:, slot, 1:2], EPS, None,
                                            ALU.add).then_inc(eps_added, 1)
                    pool.wait_ge(eps_added, b * T + t + 1)
                    nc.gpsimd.tensor_tensor(rstd[:, slot:slot + 1], var_eps[:, slot:slot + 1], half[:, :],
                                            ALU.pow).then_inc(rstd_done, 1)


def kernel(x, adj, L0_gnn_Wq, L0_gnn_Wk, L0_gnn_Wv, L0_gnn_Wo):
    import numpy as np
    import concourse.bacc as bacc
    from concourse.bass_utils import run_bass_kernel_spmd

    pick = np.zeros((4, J, 4, J, HD), np.float32)
    for t in range(4):
        for j in range(J):
            pick[t, j, t, j] = 1
    arrays = {
        "x": np.ascontiguousarray(x), "adj": np.ascontiguousarray(adj),
        "wqT": np.ascontiguousarray(np.transpose(L0_gnn_Wq)), "wkT": np.ascontiguousarray(np.transpose(L0_gnn_Wk)),
        "wvT": np.ascontiguousarray(np.transpose(L0_gnn_Wv)), "woT": np.ascontiguousarray(np.transpose(L0_gnn_Wo)),
        "ident": np.eye(P, dtype=np.float32), "pick": pick.reshape(4 * J, 4, P),
    }
    arrays = {f"in_{n}": a for n, a in arrays.items()}
    nc = bacc.Bacc("TRN2", target_bir_lowering=False, num_devices=1)
    aps = [nc.dram_tensor(n, a.shape, mybir.dt.from_np(a.dtype), kind="ExternalInput").ap() for n, a in arrays.items()]
    out = nc.dram_tensor("out", (B, N, D), F32, kind="ExternalOutput").ap()
    adj_gnn(nc, *aps, out)
    r = run_bass_kernel_spmd(nc, [arrays], core_ids=[0])
    return r.results[0]["out"]
```

```python
from contextlib import ExitStack

import concourse.bass as bass
from concourse import mybir

F32 = mybir.dt.float32
F32R = mybir.dt.float32r
ALU = mybir.AluOpType
ACT = mybir.ActivationFunctionType

P = 128
B, N, D = 8, 1024, 512
H = 16
HD = D // H
J = P // HD
G = H // J
T = N // P
KC = D // P
SLOTS = T * 8
BSLOTS = G * SLOTS
STEPS = G * T * J
EPS = 1e-5
SCALE = D ** -0.5
BIG = 3.0e38

T_LAG = 10
PV_LAG = 12
DVE_BLOCKS = (0, 3, 6)
TAIL = PV_LAG + 5


def plan():
    def four(s):
        return s, s + 1, s + 2, s + 3

    def two(s):
        return s, s, s + 1, s + 1

    parts = []
    for g in range(G):
        if g == 0:
            where = {("q", 1): two(1), ("rT", 1): (11,), ("rB", 1): (13,), ("k", 0): two(15), ("vT", 0): two(21),
                     ("v", 0): (24,), ("k", 1): two(29), ("vT", 1): two(35), ("v", 1): (38,), ("q", 0): two(43),
                     ("rT", 0): (47,), ("rB", 0): (49,)}
            for t in range(T):
                where["o", t] = two((4, 6, 8, 18, 26, 32, 40, 52)[t])
        elif g == G - 1:
            where = {("q", 1): two(1), ("k", 0): four(15), ("k", 1): four(31), ("rT", 1): (37,), ("rB", 1): (39,),
                     ("vT", 0): two(41), ("v", 0): (44,), ("q", 0): four(46), ("vT", 1): four(53), ("v", 1): (58,),
                     ("rT", 0): (59,), ("rB", 0): (61,)}
            for t in range(T):
                where["hT", t] = ((4, 6, 8, 10, 22, 24, 26, 28)[t],)
        else:
            where = {("q", 1): four(1), ("rT", 1): (9,), ("rB", 1): (13,), ("k", 0): four(15), ("vT", 0): four(21),
                     ("v", 0): (26,), ("k", 1): four(29), ("vT", 1): four(35), ("v", 1): (40,), ("q", 0): four(43),
                     ("rT", 0): (49,), ("rB", 0): (51,)}
        for unit, slots in sorted(where.items(), key=lambda kv: kv[1][0]):
            for p, s in enumerate(slots):
                parts.append((g * SLOTS + s, g, unit, p, p == len(slots) - 1))
    return parts


PLAN = plan()


def exists(g, unit, first, last):
    if first and g == 0 and (unit[0] == "o" or unit in (("rT", 1), ("rB", 1))):
        return False
    if first and g == 0 and unit == ("q", 1):
        return False
    return not (last and g == G - 1 and (unit == ("q", 0) or unit[0] in ("hT", "k", "vT", "v")))


def ranks(first, last):
    order = [(g, u) for _, g, u, p, _ in PLAN if p == 0 and exists(g, u, first, last)]
    return {x: n for n, x in enumerate(order)}


RANK = {(f, la): ranks(f, la) for f in (False, True) for la in (False, True)}
NORM_AT = [tuple(2 * SLOTS + 17 + 8 * t + n for n in (0, 1, 3)) for t in range(4)] + [
    tuple((G - 1) * SLOTS + 13 + 2 * (t - 4) + n for n in (0, 1, 4)) for t in range(4, T)]
INVERT_STEPS = 5
UNITS = len(RANK[False, False])
FIRST_UNITS = len(RANK[True, False])
HEAD = ([("hT", t) for t in range(4)] + [("k", 0)] + [("hT", t) for t in range(4, T)]
        + [("k", 1), ("q", 0), ("q", 1), ("vT", 0), ("v", 0), ("vT", 1), ("v", 1)])
SPLIT_AT = {0: "k", HEAD.index(("k", 0)): "q", HEAD.index(("q", 1)): "v"}
HEAD_UNITS = len(HEAD)
W_ORDER = "kvq"
FIRST_ORDER = "kqv"
SPLIT = ("hT", "k", "q")
HEAD_SPLITS = sum(u[0] in SPLIT for u in HEAD)
SPLITS = [x for x in RANK[False, False] if x[1][0] in SPLIT]
LACK = UNITS - FIRST_UNITS


def fed(b, g, unit):
    if unit == ("q", 1):
        return b, g
    return (b, g + 1) if g + 1 < G else (b + 1, 0)


def adj_gnn(nc, x, adj, wq, wk, wv, wo, ident_in, pick_in, out):
    with ExitStack() as ctx:
        def sb(name, shape, dt=F32):
            return ctx.enter_context(nc.sbuf_tensor(name, shape, dt))

        def psum(name, shape):
            return ctx.enter_context(nc.psum_tensor(name, shape, F32))

        def sem(name):
            return ctx.enter_context(nc.semaphore(name))

        ident = sb("ident", [P, P])
        pick = sb("pick", [32, 4, P], F32R)
        half = sb("half", [P, 1])
        w_part = sb("w_part", [P, 2, 2, KC, P], F32R)
        wo_sb = sb("wo_sb", [P, KC, D])
        xbuf = sb("xbuf", [P, 4, D])
        stats = sb("stats", [P, 6])
        moments = sb("moments", [P, 4, 2])
        rstd = sb("rstd", [P, 4])
        var_eps = sb("var_eps", [P, 4])
        hT_hi = sb("hT_hi", [P, KC, N], F32R)
        hT_lo = sb("hT_lo", [P, KC, N], F32R)
        part_hi = sb("part_hi", [P, D], F32R)
        part_lo = sb("part_lo", [P, D], F32R)
        k_stack = sb("k_stack", [P, 2, J, N], F32R)
        q_stack = sb("q_stack", [P, J, N], F32R)
        v_sb = sb("v_sb", [P, 2, T, P])
        adj_sb = sb("adj_sb", [P, T, N])
        probs = sb("probs", [P, 2, J, N])
        probsT = sb("probsT", [P, 4, J * P])
        neg_max = sb("neg_max", [P, 2, T * J])
        row_sum = sb("row_sum", [P, 2, T * J])
        keep = sb("keep", [P, 16])
        rinv_parts = sb("rinv_parts", [P, 32], F32R)
        rT = sb("rT", [32, P], F32R)
        oT = sb("oT", [P, G, N])

        scores = psum("scores", [P, 2, N])
        blockT = psum("blockT", [P, 2, J * P])
        o_acc = psum("o_acc", [P, D])
        side = psum("side", [P, D])

        w_split = {n: nc.dram_tensor(f"w{n}_split", (P, 2, KC, D), F32, kind="Internal").ap() for n in "qkv"}

        def chunks(room):
            return room.rearrange("p a (c o) -> p (a c) o", o=D)

        w_whole = {"k": chunks(probs[:, 1, 0:2, :]), "v": chunks(probs[:, 0, 2:4, :]),
                   "q": chunks(probs[:, 0, 0:2, :])}
        w_first = {"k": (chunks(k_stack[:, 1, 0:2, :]), chunks(k_stack[:, 1, 2:4, :])),
                   "q": (chunks(q_stack[:, 0:2, :]), chunks(q_stack[:, 2:4, :]))}
        w_first["v"] = w_first["k"]
        pick_whole = probs[0:32, 1, 2, 0:4 * P].rearrange("p (t o) -> p t o", o=P)
        part = part_hi[:, :], part_lo[:, :]
        first_part = {("k", 0): part, ("q", 1): part,
                      ("q", 0): tuple(probs[:, 1, 0, c * D:(c + 1) * D].bitcast(F32R) for c in range(2)),
                      ("k", 1): tuple(probs[:, 1, 1, c * D:(c + 1) * D].bitcast(F32R) for c in range(2))}

        const_loaded = sem("const_loaded")
        w_arrived = {n: sem(f"w{n}_arrived") for n in "qkv"}
        w_hi_set = sem("w_hi_set")
        w_lo_set = sem("w_lo_set")
        w_kept = {n: sem(f"w{n}_kept") for n in "qkv"}
        pick_loaded = sem("pick_loaded")
        pick_set = sem("pick_set")
        half_set = sem("half_set")
        passed = sem("passed")
        wo_loaded = sem("wo_loaded")
        w_loaded = [sem(f"w_loaded{i}") for i in range(2)]
        adj_loaded = [sem(f"adj_loaded{t}") for t in range(T)]
        x_loaded = [sem(f"x_loaded{i}") for i in range(4)]
        stats_done = sem("stats_done")
        moments_done = sem("moments_done")
        eps_added = sem("eps_added")
        rstd_done = sem("rstd_done")
        normed = sem("normed")
        side_computed = sem("side_computed")
        hi_split = sem("hi_split")
        side_retired = sem("side_retired")
        k_stacked = [[sem(f"k_stacked{c}{j}") for j in range(J)] for c in range(2)]
        q_stacked = [[sem(f"q_stacked{c}{j}") for j in range(J)] for c in range(2)]
        qk_done = sem("qk_done")
        max_done = sem("max_done")
        exp_done = sem("exp_done")
        block_done = sem("block_done")
        act_brought = sem("act_brought")
        dve_brought = sem("dve_brought")
        pv_done = sem("pv_done")
        o_brought = sem("o_brought")
        r_step = sem("r_step")
        r_ready = sem("r_ready")
        y_stored = [sem(f"y_stored{i}") for i in range(4)]

        block = ctx.enter_context(nc.Block())

        def wait(eng, s, value):
            if not isinstance(value, int) or value > 0:
                eng.wait_ge(s, value)

        def wait_apart(eng, s, value):
            wait(eng, s, value)
            if not isinstance(value, int):
                eng.sem_inc(passed, 1)

        def unit_index(b, first, last, g, unit):
            r = RANK[first, last][g, unit]
            if first:
                return HEAD_UNITS + r
            return b * UNITS + (HEAD_UNITS - LACK) + r

        def split_index(b, g, unit):
            return HEAD_SPLITS - 1 + b * len(SPLITS) + SPLITS.index((g, unit))

        def w_slot(g, n):
            return (g * 3 + W_ORDER.index(n) - 3) % 2

        def w_count(b, g, n):
            return (b * (G * 3 // 2) + (g * 3 + W_ORDER.index(n) - 3) // 2 + 1) * 16

        def end_index(n):
            return (B - 1) * UNITS + (HEAD_UNITS - LACK) + len(RANK[False, True]) + n

        def brought(eng, i_tile, mi):
            if mi in DVE_BLOCKS:
                wait(eng, dve_brought, i_tile * len(DVE_BLOCKS) + DVE_BLOCKS.index(mi) + 1)
            else:
                acts = [m for m in range(8) if m not in DVE_BLOCKS]
                wait(eng, act_brought, i_tile * len(acts) + acts.index(mi) + 1)

        def bodies(eng, body, tail):
            body(0, True, False)
            with eng.Fori(1, B - 1) as b:
                body(b, False, False)
            body(B - 1, False, True)
            tail()

        def units_ending(kap, first, last):
            return [(g, u) for s, g, u, _, end in PLAN if s == kap and end and exists(g, u, first, last)]

        @block.sync
        def _(sp):
            def load_x(b, t, after_norm):
                if after_norm:
                    if t >= 4:
                        wait_apart(sp, y_stored[t % 4], (b * 2 + 1) * 16)
                sp.dma_start(xbuf[:, t % 4, :], x[b, t * P:(t + 1) * P, :]).then_inc(x_loaded[t % 4], 16)

            def load_w(g, n):
                slot = w_slot(g, n)
                sp.dma_start(w_part[:, slot].bitcast(F32), w_split[n][:, :, :, g * P:(g + 1) * P]).then_inc(w_loaded[slot], 16)

            def stack_k(buf, c, index, parts=part):
                hi, lo = parts
                wait_apart(sp, side_retired, index + 1)
                for j in range(J):
                    for quad, rows in enumerate((hi, lo, hi, lo)):
                        sp.dma_start(k_stack[quad * HD:(quad + 1) * HD, buf, j, c * D:(c + 1) * D].bitcast(F32),
                                     rows[j * HD:(j + 1) * HD, :].bitcast(F32)).then_inc(k_stacked[c][j], 16)

            def stack_q(c, index, used, parts=part):
                hi, lo = parts
                wait_apart(sp, side_retired, index + 1)
                wait_apart(sp, qk_done, used)
                for j in range(J):
                    for quad, rows in enumerate((hi, hi, lo, lo)):
                        sp.dma_start(q_stack[quad * HD:(quad + 1) * HD, j, c * D:(c + 1) * D].bitcast(F32),
                                     rows[j * HD:(j + 1) * HD, :].bitcast(F32)).then_inc(q_stacked[c][j], 16)

            def keep_w(n):
                i = FIRST_ORDER.index(n)
                for half_of, done in enumerate((w_hi_set, w_lo_set)):
                    wait(sp, done, i + 1)
                    sp.dma_start(w_split[n][:, half_of], w_first[n][half_of].bitcast(F32)).then_inc(w_kept[n], 16)

            def store_y(b, t, index):
                wait_apart(sp, side_retired, index + 1)
                sp.dma_start(out[b, t * P:(t + 1) * P, :], xbuf[:, t % 4, :]).then_inc(y_stored[t % 4], 16)

            sp.dma_start(ident[:, :], ident_in).then_inc(const_loaded, 16)
            for t in range(4):
                load_x(0, t, False)
            for n in FIRST_ORDER:
                w = {"q": wq, "k": wk, "v": wv}[n]
                sp.dma_start(w_whole[n], w.rearrange("(c p) o -> p c o", p=P)).then_inc(w_arrived[n], 16)
            sp.dma_start(pick_whole, pick_in).then_inc(pick_loaded, 16)
            for t in range(4, T):
                wait(sp, side_computed, HEAD.index(("hT", t - 4)) + 1)
                load_x(0, t, False)
            stack_k(0, 0, HEAD.index(("k", 0)))
            keep_w("k")
            keep_w("q")
            for t in range(T):
                sp.dma_start(adj_sb[:, t, :], adj[0, t * P:(t + 1) * P, :]).then_inc(adj_loaded[t], 16)
            stack_k(0, 1, HEAD.index(("k", 1)), first_part["k", 1])
            wait(sp, side_computed, HEAD.index(("q", 1)) + 1)
            wait(sp, w_kept["q"], 32)
            stack_q(0, HEAD.index(("q", 0)), 0, first_part["q", 0])
            wait(sp, w_kept["k"], 32)
            load_w(1, "k")
            stack_q(1, HEAD.index(("q", 1)), 0)
            keep_w("v")
            sp.dma_start(wo_sb[:, :, :], wo.rearrange("(c p) o -> p c o", p=P)).then_inc(wo_loaded, 16)
            wait(sp, w_kept["v"], 32)
            load_w(1, "v")
            wait(sp, side_computed, HEAD.index(("vT", 1)) + 1)

            def body(b, first, last):
                for kap in range(BSLOTS):
                    g, lam = kap // SLOTS, kap % SLOTS
                    for gu, u in units_ending(kap - 1, first, last):
                        index = unit_index(b, first, last, gu, u)
                        bf, gf = fed(b, gu, u)
                        if u in (("k", 1), ("q", 1), ("vT", 1)):
                            nb, ng, nn = bf, gf, {"k": "q", "vT": "k", "q": "v"}[u[0]]
                            if u[0] != "k":
                                nb, ng = (bf, gf + 1) if gf + 1 < G else (bf + 1, 0)
                            if not (last and (ng == 0)):
                                wait_apart(sp, side_computed, index + 1)
                                load_w(ng, nn)
                        if u[0] == "k":
                            stack_k((gu + 1) % 2, u[1], index)
                        if u[0] == "q":
                            stack_q(u[1], index, b * STEPS + gu * T * J + (T * J // 2 if u[1] == 0 else 0))
                        if u[0] == "o":
                            store_y(b - 1, u[1], index)
                            if u[1] < 4:
                                load_x(b - 1, u[1] + 4, True)
                        if u[0] == "hT" and u[1] < 4:
                            wait_apart(sp, side_computed, index + 1)
                            load_x(b + 1, u[1] + 4, False)
                    if g == G - 1 and not last and lam % 8 == 7:
                        t = lam // 8
                        wait_apart(sp, max_done, b * STEPS + (g * T + t) * J + J)
                        sp.dma_start(adj_sb[:, t, :], adj[b + 1, t * P:(t + 1) * P, :]).then_inc(adj_loaded[t], 16)
                    if g == 1 and lam in (10, 12, 14, 16) and not last:
                        t = (lam - 10) // 2
                        if not first:
                            wait_apart(sp, y_stored[t], b * 2 * 16)
                        load_x(b + 1, t, False)
                    if g == G - 1 and lam in (52, 54, 56, 58):
                        t = (lam - 52) // 2
                        if last:
                            wait_apart(sp, y_stored[t], b * 2 * 16)
                        else:
                            wait_apart(sp, side_computed, unit_index(b, first, last, g, ("hT", t + 4)) + 1)
                        load_x(b, t, True)

            def tail():
                for t in range(T):
                    store_y(B - 1, t, end_index(2 + t))
                    if t < 4:
                        load_x(B - 1, t + 4, True)
                for i in range(4):
                    wait_apart(sp, y_stored[i], B * 2 * 16)

            bodies(sp, body, tail)

        @block.tensor
        def _(pe):
            def side_part(b, g, unit, p, end, index, head=False):
                kind, c = unit
                if p == 0:
                    wait(pe, side_retired, index)
                if kind == "hT":
                    wait(pe, normed, b * T + c + 1)
                    for i in range(KC):
                        last = nc.tensor.transpose(side[:, i * P:(i + 1) * P],
                                                   xbuf[:, c % 4, i * P:(i + 1) * P], ident[:, :])
                elif kind in ("k", "q", "vT"):
                    n = kind[0]
                    slot = w_slot(g, n)
                    if head:
                        if p == 0:
                            wait(pe, w_hi_set, FIRST_ORDER.index(n) + 1)
                            wait(pe, w_lo_set, FIRST_ORDER.index(n) + 1)
                        weights = [w_first[n][w][:, p, 0:P] for w in range(2)]
                    else:
                        if p == 0 and unit != ("q", 1):
                            wait(pe, w_loaded[slot], w_count(b, g, n))
                        weights = [w_part[:, slot, w, p, :] for w in range(2)]
                    for i, (w, h) in enumerate(((0, hT_hi), (0, hT_lo), (1, hT_hi))):
                        last = nc.tensor.matmul(side[:, :], weights[w], h[:, p, c * D:(c + 1) * D],
                                                start=p == 0 and i == 0, stop=p == KC - 1 and i == 2)
                elif kind == "v":
                    for i in range(4):
                        last = nc.tensor.transpose(side[:, i * P:(i + 1) * P], v_sb[:, g % 2, c * 4 + i, :],
                                                   ident[:, :])
                elif kind == "rT":
                    wait(pe, r_ready, b * G * 2 + g * 2 + c + 1)
                    last = nc.tensor.transpose(side[0:32, 0:P], rinv_parts[:, :].bitcast(F32), ident[:, :])
                elif kind == "rB":
                    for i in range(4):
                        last = nc.tensor.matmul(side[:, i * P:(i + 1) * P], pick[:, i, :], rT[:, :],
                                                start=True, stop=True)
                elif kind == "o":
                    if p == 0 and c == 0:
                        wait(pe, wo_loaded, 16)
                    last = nc.tensor.matmul(side[:, :], oT[:, p, c * P:(c + 1) * P], wo_sb[:, p, :],
                                            start=p == 0, stop=p == KC - 1)
                if end:
                    last.then_inc(side_computed, 1)

            def transposes(tile, t, mi):
                if mi == 0:
                    wait(pe, exp_done, tile * J + J)
                if mi >= 2:
                    brought(pe, tile, mi - 2)
                else:
                    brought(pe, tile - 1, mi + 6)
                for j in range(J):
                    last = nc.tensor.transpose(blockT[:, mi % 2, j * P:(j + 1) * P],
                                               probs[:, t % 2, j, mi * P:(mi + 1) * P], ident[:, :])
                last.then_inc(block_done, 1)

            def products(tile, half_index, gi, t, mi):
                brought(pe, tile, mi)
                if mi == 0 and t % 4 == 0:
                    wait(pe, o_brought, half_index)
                for j in range(J):
                    last = nc.tensor.matmul(o_acc[j * HD:(j + 1) * HD, (t % 4) * P:(t % 4 + 1) * P],
                                            v_sb[:, gi % 2, mi, j * HD:(j + 1) * HD],
                                            probsT[:, mi % 4, j * P:(j + 1) * P],
                                            start=mi == 0, stop=mi == 7, tile_position=(0, j * HD))
                last.then_inc(pv_done, 1)

            wait(pe, const_loaded, 16)
            for n, unit in enumerate(HEAD):
                for p in range(1 if unit[0] in ("hT", "v") else 4):
                    side_part(0, 0, unit, p, unit[0] in ("hT", "v") or p == 3, n, head=True)

            def body(b, first, last):
                for kap in range(BSLOTS + (TAIL if last else 0)):
                    g, t, mi = kap // SLOTS, kap % SLOTS // 8, kap % 8
                    if kap < BSLOTS and mi % 2 == 0:
                        j = mi // 2
                        s = kap // 2
                        if t == 0:
                            for c in range(2):
                                wait(pe, k_stacked[c][j], (b * G + g + 1) * 16 * 4)
                        if t % 4 == 0:
                            wait(pe, q_stacked[t // 4][j], (b * G + g + 1) * 16 * 4)
                        wait(pe, exp_done, b * STEPS + s - 1)
                        for c in range(2):
                            mm = nc.tensor.matmul(scores[:, s % 2, c * D:(c + 1) * D],
                                                  q_stack[:, j, t * P:(t + 1) * P],
                                                  k_stack[:, g % 2, j, c * D:(c + 1) * D], start=True, stop=True)
                        mm.then_inc(qk_done, 1)
                    i = kap - T_LAG
                    if not (first and i < 0) and i < BSLOTS:
                        transposes(b * G * T + i // 8, i // 8 % T, i % 8)
                    for s, gu, u, p, end in PLAN:
                        if s != kap or not exists(gu, u, first, last):
                            continue
                        if u[0] == "hT":
                            bb, gg = b + 1, 0
                        elif u[0] in ("k", "q", "vT", "v"):
                            bb, gg = fed(b, gu, u)
                        elif u in (("rT", 1), ("rB", 1)):
                            bb, gg = b, gu - 1
                        else:
                            bb, gg = b, gu
                        side_part(bb, gg, u, p, end, unit_index(b, first, last, gu, u))
                    if kap % 2 == PV_LAG % 2:
                        continue
                    for i in (kap - PV_LAG - 1, kap - PV_LAG):
                        if not (first and i < 0) and i < BSLOTS:
                            products(b * G * T + i // 8, b * G * 2 + i // 32, i // SLOTS % G, i // 8 % T, i % 8)

            def tail():
                for n, unit in enumerate([("rT", 1), ("rB", 1)] + [("o", t) for t in range(T)]):
                    for p in range(4 if unit[0] == "o" else 1):
                        side_part(B - 1, G - 1, unit, p, unit[0] != "o" or p == 3, end_index(n))

            wait(pe, pick_set, 1)
            bodies(pe, body, tail)

        @block.scalar
        def _(act):
            def retire(b, g, unit, index, hi=part[0], head=False):
                kind, c = unit
                if kind == "hT":
                    act.wait_ge(side_computed, index + 1)
                    nc.scalar.activation(hT_hi[:, :, c * P:(c + 1) * P],
                                         side[:, :].rearrange("p (i n) -> p i n", i=KC), ACT.Relu
                                         ).then_inc(hi_split, 1)
                elif kind == "vT":
                    act.wait_ge(side_computed, index + 1)
                    nc.scalar.activation(v_sb[:, g % 2, c * 4:(c + 1) * 4, :],
                                         side[:, :].rearrange("p (i n) -> p i n", i=4), ACT.Copy
                                         ).then_inc(side_retired, 1)
                elif kind == "v":
                    act.wait_ge(side_computed, index + 1)
                    nc.scalar.activation(v_sb[:, g % 2, c * 4:(c + 1) * 4, :],
                                         side[:, :].rearrange("p (i n) -> p i n", i=4), ACT.Copy
                                         ).then_inc(side_retired, 1)
                elif kind == "k":
                    act.wait_ge(side_computed, index + 1)
                    if head:
                        wait(act, w_lo_set, c)
                    elif c == 0:
                        stacked(q_stacked[1], b * G + g)
                    else:
                        stacked(k_stacked[0], b * G + g + 1)
                    nc.scalar.activation(hi, side[:, :], ACT.Copy).then_inc(hi_split, 1)
                elif kind == "q":
                    act.wait_ge(side_computed, index + 1)
                    if head:
                        if c == 0:
                            wait(act, w_lo_set, 1)
                        else:
                            stacked(k_stacked[0], 1)
                    else:
                        stacked(k_stacked[1] if c == 0 else q_stacked[0], b * G + g + 1)
                    nc.scalar.activation(hi, side[:, :], ACT.Copy, scale=SCALE / 2).then_inc(hi_split, 1)

            def stacked(parts, count):
                for j in range(J):
                    wait(act, parts[j], count * 16 * 4)

            def bring(tile, mi):
                act.wait_ge(block_done, tile * 8 + mi + 1)
                wait(act, pv_done, tile * 8 + mi - 3)
                nc.scalar.activation(probsT[:, mi % 4, :], blockT[:, mi % 2, :], ACT.Copy).then_inc(act_brought, 1)

            def bring_o(half_index, pv_count, o_used):
                act.wait_ge(pv_done, pv_count)
                wait(act, side_computed, o_used)
                nc.scalar.activation(oT[:, half_index // 2 % G, half_index % 2 * D:(half_index % 2 + 1) * D],
                                     o_acc[:, :], ACT.Copy).then_inc(o_brought, 1)

            def split_w(n):
                wait(act, w_arrived[n], 16)
                if n == "v":
                    wait(act, w_kept["k"], 32)
                nc.scalar.activation(w_first[n][0], w_whole[n], ACT.Copy).then_inc(w_hi_set, 1)

            for n, unit in enumerate(HEAD):
                if n in SPLIT_AT:
                    split_w(SPLIT_AT[n])
                retire(0, 0, unit, n, first_part.get(unit, part)[0], head=True)

            def body(b, first, last):
                for kap in range(BSLOTS + (TAIL if last else 0)):
                    g, t, mi = kap // SLOTS, kap % SLOTS // 8, kap % 8
                    i = kap - T_LAG
                    if i % 8 not in DVE_BLOCKS and not (first and i < 0) and i < BSLOTS:
                        bring(b * G * T + i // 8, i % 8)
                    if kap < BSLOTS and mi % 2 == 1:
                        j, s = mi // 2, kap // 2
                        act.wait_ge(max_done, b * STEPS + s + 1)
                        if j == 0:
                            wait(act, block_done, (b * G * T + g * T + t - 1) * 8)
                        nc.scalar.activation(probs[:, t % 2, j, :], scores[:, s % 2, :], ACT.Exp,
                                             bias=neg_max[:, g % 2, t * J + j:t * J + j + 1], scale=-1.0,
                                             accum_out=row_sum[:, g % 2, t * J + j:t * J + j + 1]
                                             ).then_inc(exp_done, 1)
                    i = kap - PV_LAG
                    if i % 32 == 31 and not (first and i < 0) and i < BSLOTS:
                        hh = i // 32
                        o_used = 0
                        if hh in (0, 1) and not first:
                            o_used = unit_index(b, first, last, 0, ("o", 4 * hh + 3)) + 1
                        bring_o(hh, (b * BSLOTS) + i + 1, o_used)
                    for gu, u in units_ending(kap, first, last):
                        bb, gg = fed(b, gu, u) if u[0] in ("k", "q", "vT", "v") else (b, gu)
                        retire(bb, gg, u, unit_index(b, first, last, gu, u))

            bodies(act, body, lambda: None)

        @block.vector
        def _(dve):
            def norm_stats(b, t):
                slot = t % 4
                wait_apart(dve, moments_done, b * T + t)
                dve.wait_ge(x_loaded[slot], norm_loads(b, t))
                nc.vector.bn_stats(stats[:, :], xbuf[:, slot, :]).then_inc(stats_done, 1)

            def norm_moments(b, t):
                slot = t % 4
                wait_apart(dve, stats_done, b * T + t + 1)
                nc.vector.bn_aggr(moments[:, slot, :], stats[:, :]).then_inc(moments_done, 1)

            def norm_loads(b, t):
                before = 0 if isinstance(b, int) and b == 0 else 4 * b - 2
                return (before + t // 4 + 1) * 16

            def normalise(b, t):
                slot = t % 4
                dve.wait_ge(rstd_done, b * T + t + 1)
                nc.vector.tensor_scalar(xbuf[:, slot, :], xbuf[:, slot, :], moments[:, slot, 0:1],
                                        rstd[:, slot:slot + 1], ALU.subtract, ALU.mult).then_inc(normed, 1)

            def retire(b, g, unit, index, split=0, parts=part):
                kind, c = unit
                if kind in ("k", "q"):
                    dve.wait_ge(hi_split, split + 1)
                    nc.vector.scalar_tensor_tensor(parts[1], side[:, :], 1.0 if kind == "k" else SCALE / 2,
                                                   parts[0].bitcast(F32), ALU.mult, ALU.subtract
                                                   ).then_inc(side_retired, 1)
                elif kind == "hT":
                    dve.wait_ge(hi_split, split + 1)
                    nc.vector.scalar_tensor_tensor(hT_lo[:, :, c * P:(c + 1) * P],
                                                   side[:, :].rearrange("p (i n) -> p i n", i=KC), 0.0,
                                                   hT_hi[:, :, c * P:(c + 1) * P].bitcast(F32),
                                                   ALU.max, ALU.subtract).then_inc(side_retired, 1)
                elif kind == "rT":
                    dve.wait_ge(side_computed, index + 1)
                    nc.vector.tensor_copy(rT[:, :], side[0:32, 0:P]).then_inc(side_retired, 1)
                elif kind == "rB":
                    dve.wait_ge(side_computed, index + 1)
                    dve.wait_ge(o_brought, (b * G + g) * 2 + c + 1)
                    o_half = oT[:, g % G, c * D:(c + 1) * D]
                    nc.vector.tensor_tensor(o_half, side[:, :], o_half, ALU.mult).then_inc(side_retired, 1)
                elif kind == "o":
                    dve.wait_ge(side_computed, index + 1)
                    dve.wait_ge(x_loaded[c % 4], sum_loads(b, c))
                    nc.vector.tensor_tensor(xbuf[:, c % 4, :], side[:, :], xbuf[:, c % 4, :],
                                            ALU.add).then_inc(side_retired, 1)

            def sum_loads(b, t):
                if isinstance(b, int) and b == B - 1:
                    return (b * 4 + 2 + t // 4 + 1) * 16
                return (b * 4 + 4 + t // 4 + 1) * 16

            def invert(b, g, c, transposed, step):
                half_index = (b * G + g) * 2 + c
                cols = slice(16 * c, 16 * c + 16)
                rinv_hi = rinv_parts[:, 0:16]
                rinv_lo = rinv_parts[:, 16:32]
                rinv = rinv_lo.bitcast(F32)
                if step > 0:
                    dve.wait_ge(r_step, half_index * 5 + 1 + step)
                if step == 0:
                    dve.wait_ge(exp_done, (b * G + g) * T * J + 16 * (c + 1))
                    wait(dve, side_computed, transposed)
                    nc.vector.reciprocal(rinv, row_sum[:, g % 2, cols]).then_inc(r_step, 1)
                    nc.vector.tensor_scalar(keep[:, :], neg_max[:, g % 2, cols], 0.0, None,
                                            ALU.not_equal).then_inc(r_step, 1)
                if step == 1:
                    nc.vector.scalar_tensor_tensor(keep[:, :], row_sum[:, g % 2, cols], float(N), keep[:, :],
                                                   ALU.is_lt, ALU.max).then_inc(r_step, 1)
                if step == 2:
                    nc.vector.tensor_tensor(rinv, rinv, keep[:, :], ALU.mult).then_inc(r_step, 1)
                if step == 3:
                    nc.vector.tensor_copy(rinv_hi, rinv).then_inc(r_step, 1)
                if step == 4:
                    nc.vector.tensor_tensor(rinv_lo, rinv, rinv_hi.bitcast(F32), ALU.subtract).then_inc(r_ready, 1)

            nc.vector.memset(half[:, :], -0.5).then_inc(half_set, 1)

            def split_w(n):
                dve.wait_ge(w_hi_set, FIRST_ORDER.index(n) + 1)
                nc.vector.tensor_tensor(w_first[n][1], w_whole[n], w_first[n][0].bitcast(F32), ALU.subtract
                                        ).then_inc(w_lo_set, 1)

            def retire_head(n):
                unit = HEAD[n]
                retire(0, 0, unit, n, sum(u[0] in SPLIT for u in HEAD[:n]), first_part.get(unit, part))

            norm_stats(0, 0)
            norm_moments(0, 0)
            for t in range(4):
                if t < 3:
                    norm_stats(0, t + 1)
                    norm_moments(0, t + 1)
                normalise(0, t)
            retire_head(0)
            split_w("k")
            retire_head(1)
            norm_stats(0, 4)
            norm_moments(0, 4)
            retire_head(2)
            normalise(0, 4)
            norm_stats(0, 5)
            norm_moments(0, 5)
            retire_head(3)
            normalise(0, 5)
            norm_stats(0, 6)
            norm_moments(0, 6)
            retire_head(4)
            normalise(0, 6)
            norm_stats(0, 7)
            norm_moments(0, 7)
            normalise(0, 7)
            split_w("q")
            dve.wait_ge(pick_loaded, 16)
            nc.vector.tensor_copy(pick[:, :, :], pick_whole).then_inc(pick_set, 1)
            for n in range(5, HEAD_UNITS):
                if n in SPLIT_AT:
                    split_w(SPLIT_AT[n])
                retire_head(n)

            def body(b, first, last):
                for kap in range(BSLOTS + (TAIL if last else 0)):
                    g, t, mi = kap // SLOTS, kap % SLOTS // 8, kap % 8
                    lam = kap % SLOTS
                    if kap < BSLOTS and mi % 2 == 0:
                        j, s = mi // 2, kap // 2
                        wait_apart(dve, qk_done, b * STEPS + s + 1)
                        if g == 0 and j == 0:
                            wait_apart(dve, adj_loaded[t], (b + 1) * 16)
                        nc.vector.tensor_tensor_reduce(
                            out=scores[:, s % 2, :], in0=scores[:, s % 2, :], in1=adj_sb[:, t, :], scale=-2.0,
                            scalar=BIG, op0=ALU.add, op1=ALU.min,
                            accum_out=neg_max[:, g % 2, t * J + j:t * J + j + 1]).then_inc(max_done, 1)
                    i = kap - T_LAG
                    if i % 8 in DVE_BLOCKS and not (first and i < 0) and i < BSLOTS:
                        tile, m = b * G * T + i // 8, i % 8
                        dve.wait_ge(block_done, tile * 8 + m + 1)
                        wait(dve, pv_done, tile * 8 + m - 3)
                        nc.vector.tensor_copy(probsT[:, m % 4, :], blockT[:, m % 2, :]).then_inc(dve_brought, 1)
                    for s, gu, u, _, _ in PLAN:
                        step = kap - (s - INVERT_STEPS - 1)
                        if u[0] == "rT" and 0 <= step < INVERT_STEPS and exists(gu, u, first, last):
                            gg = gu - 1 if u[1] == 1 else gu
                            invert(b, gg, u[1], rt_last(b, first, last, gu, u), step)
                    step = kap - (BSLOTS + 7)
                    if last and 0 <= step < INVERT_STEPS:
                        invert(b, G - 1, 1, unit_index(b, first, last, G - 1, ("rT", 0)) + 1, step)
                    if not last:
                        for t2, slots in enumerate(NORM_AT):
                            for step, s in zip((norm_stats, norm_moments, normalise), slots):
                                if s == kap:
                                    step(b + 1, t2)
                    for gu, u in units_ending(kap, first, last):
                        bb, gg = (b, gu)
                        if u[0] in ("k", "q", "vT", "v"):
                            bb, gg = fed(b, gu, u)
                        elif u[0] == "hT":
                            bb = b + 1
                        elif u[0] == "rB" and u[1] == 1:
                            bb, gg = (b, gu - 1) if gu > 0 else (b - 1, G - 1)
                        elif u[0] == "o":
                            bb = b - 1
                        retire(bb, gg, u, unit_index(b, first, last, gu, u),
                               split_index(b, gu, u) if u[0] in SPLIT else 0)

            def rt_last(b, first, last, gu, u):
                if u == ("rT", 0):
                    if first and gu == 0:
                        return 0
                    return unit_index(b, first, last, gu, ("rT", 1)) + 1
                if gu > 0:
                    return unit_index(b, first, last, gu - 1, ("rT", 0)) + 1
                return b * UNITS + (HEAD_UNITS - LACK) - (UNITS - RANK[False, False][G - 1, ("rT", 0)]) + 1

            def tail():
                retire(B - 1, G - 1, ("rT", 1), end_index(0))
                retire(B - 1, G - 1, ("rB", 1), end_index(1))
                for t in range(T):
                    retire(B - 1, G - 1, ("o", t), end_index(2 + t))

            bodies(dve, body, tail)

        @block.gpsimd
        def _(pool):
            pool.wait_ge(half_set, 1)
            with pool.Fori(0, B) as b:
                for t in range(T):
                    slot = t % 4
                    wait_apart(pool, moments_done, b * T + t + 1)
                    nc.gpsimd.tensor_scalar(var_eps[:, slot:slot + 1], moments[:, slot, 1:2], EPS, None,
                                            ALU.add).then_inc(eps_added, 1)
                    pool.wait_ge(eps_added, b * T + t + 1)
                    nc.gpsimd.tensor_tensor(rstd[:, slot:slot + 1], var_eps[:, slot:slot + 1], half[:, :],
                                            ALU.pow).then_inc(rstd_done, 1)


def kernel(x, adj, L0_gnn_Wq, L0_gnn_Wk, L0_gnn_Wv, L0_gnn_Wo):
    import numpy as np
    import concourse.bacc as bacc
    from concourse.bass_utils import run_bass_kernel_spmd

    pick = np.zeros((2, 4, J, 4, J, HD), np.float32)
    for t in range(4):
        for j in range(J):
            pick[:, t, j, t, j] = 1
    arrays = {
        "x": np.ascontiguousarray(x), "adj": np.ascontiguousarray(adj),
        "wqT": np.ascontiguousarray(np.transpose(L0_gnn_Wq)), "wkT": np.ascontiguousarray(np.transpose(L0_gnn_Wk)),
        "wvT": np.ascontiguousarray(np.transpose(L0_gnn_Wv)), "woT": np.ascontiguousarray(np.transpose(L0_gnn_Wo)),
        "ident": np.eye(P, dtype=np.float32), "pick": pick.reshape(2 * 4 * J, 4, P),
    }
    arrays = {f"in_{n}": a for n, a in arrays.items()}
    nc = bacc.Bacc("TRN2", target_bir_lowering=False, num_devices=1)
    aps = [nc.dram_tensor(n, a.shape, mybir.dt.from_np(a.dtype), kind="ExternalInput").ap() for n, a in arrays.items()]
    out = nc.dram_tensor("out", (B, N, D), F32, kind="ExternalOutput").ap()
    adj_gnn(nc, *aps, out)
    r = run_bass_kernel_spmd(nc, [arrays], core_ids=[0])
    return r.results[0]["out"]
```

```python
from contextlib import ExitStack

import concourse.bass as bass
from concourse import mybir

F32 = mybir.dt.float32
F32R = mybir.dt.float32r
ALU = mybir.AluOpType
ACT = mybir.ActivationFunctionType

P = 128
B, N, D = 8, 1024, 512
H = 16
HD = D // H
J = P // HD
G = H // J
T = N // P
KC = D // P
SLOTS = T * 8
BSLOTS = G * SLOTS
STEPS = G * T * J
EPS = 1e-5
SCALE = D ** -0.5
BIG = 3.0e38

T_LAG = 10
PV_LAG = 12
DVE_BLOCKS = (1, 3, 7)
TAIL = PV_LAG + 5


def plan():
    def four(s):
        return s, s + 1, s + 2, s + 3

    def two(s):
        return s, s, s + 1, s + 1

    parts = []
    for g in range(G):
        if g == 0:
            where = {("q", 1): two(1), ("rT", 1): (11,), ("rB", 1): (13,), ("k", 0): two(15), ("vT", 0): two(21),
                     ("v", 0): (24,), ("k", 1): two(29), ("vT", 1): two(35), ("v", 1): (38,), ("q", 0): two(43),
                     ("rT", 0): (47,), ("rB", 0): (49,)}
            for t in range(T):
                where["o", t] = two((4, 6, 8, 18, 26, 32, 40, 52)[t])
        elif g == G - 1:
            where = {("q", 1): two(1), ("k", 0): four(15), ("k", 1): four(31), ("rT", 1): (37,), ("rB", 1): (39,),
                     ("vT", 0): two(41), ("v", 0): (44,), ("q", 0): four(46), ("vT", 1): four(53), ("v", 1): (58,),
                     ("rT", 0): (59,), ("rB", 0): (61,)}
            for t in range(T):
                where["hT", t] = ((4, 6, 8, 10, 22, 24, 26, 28)[t],)
        else:
            where = {("q", 1): four(1), ("rT", 1): (9,), ("rB", 1): (13,), ("k", 0): four(15), ("vT", 0): four(21),
                     ("v", 0): (26,), ("k", 1): four(29), ("vT", 1): four(35), ("v", 1): (40,), ("q", 0): four(43),
                     ("rT", 0): (49,), ("rB", 0): (51,)}
        for unit, slots in sorted(where.items(), key=lambda kv: kv[1][0]):
            for p, s in enumerate(slots):
                parts.append((g * SLOTS + s, g, unit, p, p == len(slots) - 1))
    return parts


PLAN = plan()


def exists(g, unit, first, last):
    if first and g == 0 and (unit[0] == "o" or unit in (("rT", 1), ("rB", 1))):
        return False
    if first and g == 0 and unit == ("q", 1):
        return False
    return not (last and g == G - 1 and (unit == ("q", 0) or unit[0] in ("hT", "k", "vT", "v")))


def ranks(first, last):
    order = [(g, u) for _, g, u, p, _ in PLAN if p == 0 and exists(g, u, first, last)]
    return {unit: n for n, unit in enumerate(order)}


RANK = {(f, la): ranks(f, la) for f in (False, True) for la in (False, True)}
UNITS = len(RANK[False, False])
LACK = UNITS - len(RANK[True, False])
SPLIT = ("hT", "k", "q")
SPLITS = [gu for gu in RANK[False, False] if gu[1][0] in SPLIT]

HEAD = ([("hT", t) for t in range(4)] + [("k", 0)] + [("hT", t) for t in range(4, T)]
        + [("k", 1), ("q", 0), ("q", 1), ("vT", 0), ("v", 0), ("vT", 1), ("v", 1)])
HEAD_UNITS = len(HEAD)
HEAD_SPLITS = sum(u[0] in SPLIT for u in HEAD)
END = [("o", t) for t in range(4)] + [("rT", 1), ("rB", 1)] + [("o", t) for t in range(4, T)]

W_ORDER = "kvq"
FIRST_ORDER = "kqv"
SPLIT_AT = {2: "k", HEAD.index(("k", 0)): "q", HEAD.index(("q", 1)): "v"}

NORM_AT = [tuple(2 * SLOTS + 17 + 8 * t + n for n in (0, 1, 3)) for t in range(4)] + [
    tuple((G - 1) * SLOTS + 13 + 2 * (t - 4) + n for n in (0, 1, 4)) for t in range(4, T)]
INVERT_STEPS = 5


def fed(b, g, unit):
    if unit == ("q", 1):
        return b, g
    return (b, g + 1) if g + 1 < G else (b + 1, 0)


def adj_gnn(nc, x, adj, wq, wk, wv, wo, ident_in, pick_in, out):
    with ExitStack() as ctx:
        def sb(name, shape, dt=F32):
            return ctx.enter_context(nc.sbuf_tensor(name, shape, dt))

        def psum(name, shape):
            return ctx.enter_context(nc.psum_tensor(name, shape, F32))

        def sem(name):
            return ctx.enter_context(nc.semaphore(name))

        ident = sb("ident", [P, P])
        pick = sb("pick", [32, 4, P], F32R)
        half = sb("half", [P, 1])
        w_part = sb("w_part", [P, 2, 2, KC, P], F32R)
        wo_sb = sb("wo_sb", [P, KC, D])
        xbuf = sb("xbuf", [P, 4, D])
        stats = sb("stats", [P, 6])
        moments = sb("moments", [P, 4, 2])
        rstd = sb("rstd", [P, 4])
        var_eps = sb("var_eps", [P, 4])
        hT_hi = sb("hT_hi", [P, KC, N], F32R)
        hT_lo = sb("hT_lo", [P, KC, N], F32R)
        part_hi = sb("part_hi", [P, D], F32R)
        part_lo = sb("part_lo", [P, D], F32R)
        k_stack = sb("k_stack", [P, 2, J, N], F32R)
        q_stack = sb("q_stack", [P, J, N], F32R)
        v_sb = sb("v_sb", [P, 2, T, P])
        adj_sb = sb("adj_sb", [P, T, N])
        probs = sb("probs", [P, 2, J, N])
        probsT = sb("probsT", [P, 4, J * P])
        neg_max = sb("neg_max", [P, 2, T * J])
        row_sum = sb("row_sum", [P, 2, T * J])
        keep = sb("keep", [P, 16])
        rinv_parts = sb("rinv_parts", [P, 32], F32R)
        rT = sb("rT", [32, P], F32R)
        oT = sb("oT", [P, G, N])

        scores = psum("scores", [P, 2, N])
        blockT = psum("blockT", [P, 2, J * P])
        o_acc = psum("o_acc", [P, D])
        side = psum("side", [P, D])

        w_split = {n: nc.dram_tensor(f"w{n}_split", (P, 2, KC, D), F32, kind="Internal").ap() for n in "qkv"}

        def chunks(room):
            return room.rearrange("p a (c o) -> p (a c) o", o=D)

        w_whole = {"k": chunks(probs[:, 1, 0:2, :]), "v": chunks(probs[:, 0, 2:4, :]),
                   "q": chunks(probs[:, 0, 0:2, :])}
        w_first = {"k": (chunks(k_stack[:, 1, 0:2, :]), chunks(k_stack[:, 1, 2:4, :])),
                   "q": (chunks(q_stack[:, 0:2, :]), chunks(q_stack[:, 2:4, :]))}
        w_first["v"] = w_first["k"]
        pick_whole = probs[0:32, 1, 2, 0:4 * P].rearrange("p (t o) -> p t o", o=P)
        part = part_hi[:, :], part_lo[:, :]
        first_part = {("k", 0): part, ("q", 1): part,
                      ("q", 0): tuple(probs[:, 1, 0, c * D:(c + 1) * D].bitcast(F32R) for c in range(2)),
                      ("k", 1): tuple(probs[:, 1, 1, c * D:(c + 1) * D].bitcast(F32R) for c in range(2))}

        const_loaded = sem("const_loaded")
        w_arrived = {n: sem(f"w{n}_arrived") for n in "qkv"}
        w_hi_set = sem("w_hi_set")
        w_lo_set = sem("w_lo_set")
        w_kept = {n: sem(f"w{n}_kept") for n in "qkv"}
        pick_loaded = sem("pick_loaded")
        pick_set = sem("pick_set")
        half_set = sem("half_set")
        passed = sem("passed")
        wo_loaded = sem("wo_loaded")
        w_loaded = [sem(f"w_loaded{i}") for i in range(2)]
        adj_loaded = [sem(f"adj_loaded{t}") for t in range(T)]
        x_loaded = [sem(f"x_loaded{i}") for i in range(4)]
        stats_done = sem("stats_done")
        moments_done = sem("moments_done")
        eps_added = sem("eps_added")
        rstd_done = sem("rstd_done")
        normed = sem("normed")
        side_computed = sem("side_computed")
        hi_split = sem("hi_split")
        side_retired = sem("side_retired")
        k_stacked = [[sem(f"k_stacked{c}{j}") for j in range(J)] for c in range(2)]
        q_stacked = [[sem(f"q_stacked{c}{j}") for j in range(J)] for c in range(2)]
        qk_done = sem("qk_done")
        max_done = sem("max_done")
        exp_done = sem("exp_done")
        block_done = sem("block_done")
        act_brought = sem("act_brought")
        dve_brought = sem("dve_brought")
        pv_done = sem("pv_done")
        o_brought = sem("o_brought")
        r_step = sem("r_step")
        r_ready = sem("r_ready")
        y_stored = [sem(f"y_stored{i}") for i in range(4)]

        block = ctx.enter_context(nc.Block())

        def wait(eng, s, value):
            if not isinstance(value, int) or value > 0:
                eng.wait_ge(s, value)

        def wait_apart(eng, s, value):
            wait(eng, s, value)
            if not isinstance(value, int):
                eng.sem_inc(passed, 1)

        def unit_index(b, first, last, g, unit):
            r = RANK[first, last][g, unit]
            if first:
                return HEAD_UNITS + r
            return b * UNITS + (HEAD_UNITS - LACK) + r

        def split_index(b, g, unit):
            return HEAD_SPLITS - 1 + b * len(SPLITS) + SPLITS.index((g, unit))

        def w_slot(g, n):
            return (g * 3 + W_ORDER.index(n) - 3) % 2

        def w_count(b, g, n):
            return (b * (G * 3 // 2) + (g * 3 + W_ORDER.index(n) - 3) // 2 + 1) * 16

        def end_index(unit):
            return (B - 1) * UNITS + (HEAD_UNITS - LACK) + len(RANK[False, True]) + END.index(unit)

        def score_bank(n):
            return scores[:, n % 4 // 2, n % 2 * D:(n % 2 + 1) * D]

        def head_bank(n):
            return score_bank(n) if HEAD[n][0] in SPLIT else side[:, :]

        def end_bank(unit):
            return score_bank(unit[1]) if unit[0] == "o" else side[:, :]

        def brought(eng, i_tile, mi):
            if mi in DVE_BLOCKS:
                wait(eng, dve_brought, i_tile * len(DVE_BLOCKS) + DVE_BLOCKS.index(mi) + 1)
            else:
                acts = [m for m in range(8) if m not in DVE_BLOCKS]
                wait(eng, act_brought, i_tile * len(acts) + acts.index(mi) + 1)

        def bodies(eng, body, tail):
            body(0, True, False)
            with eng.Fori(1, B - 1) as b:
                body(b, False, False)
            body(B - 1, False, True)
            tail()

        def units_ending(tick, first, last):
            return [(g, u) for s, g, u, _, end in PLAN if s == tick and end and exists(g, u, first, last)]

        @block.sync
        def _(sp):
            def load_x(b, t, after_norm):
                if after_norm:
                    if t >= 4:
                        wait_apart(sp, y_stored[t % 4], (b * 2 + 1) * 16)
                sp.dma_start(xbuf[:, t % 4, :], x[b, t * P:(t + 1) * P, :]).then_inc(x_loaded[t % 4], 16)

            def load_adj(b, t):
                sp.dma_start(adj_sb[:, t, :], adj[b, t * P:(t + 1) * P, :]).then_inc(adj_loaded[t], 16)

            def load_w(g, n):
                slot = w_slot(g, n)
                sp.dma_start(w_part[:, slot].bitcast(F32), w_split[n][:, :, :, g * P:(g + 1) * P]
                             ).then_inc(w_loaded[slot], 16)

            def stack_k(buf, c, index, parts=part):
                hi, lo = parts
                wait_apart(sp, side_retired, index + 1)
                for j in range(J):
                    for quad, rows in enumerate((hi, lo, hi, lo)):
                        sp.dma_start(k_stack[quad * HD:(quad + 1) * HD, buf, j, c * D:(c + 1) * D].bitcast(F32),
                                     rows[j * HD:(j + 1) * HD, :].bitcast(F32)).then_inc(k_stacked[c][j], 16)

            def stack_q(c, index, used, parts=part):
                hi, lo = parts
                wait_apart(sp, side_retired, index + 1)
                wait_apart(sp, qk_done, used)
                for j in range(J):
                    for quad, rows in enumerate((hi, hi, lo, lo)):
                        sp.dma_start(q_stack[quad * HD:(quad + 1) * HD, j, c * D:(c + 1) * D].bitcast(F32),
                                     rows[j * HD:(j + 1) * HD, :].bitcast(F32)).then_inc(q_stacked[c][j], 16)

            def keep_w(n):
                i = FIRST_ORDER.index(n)
                for half_of, done in enumerate((w_hi_set, w_lo_set)):
                    wait(sp, done, i + 1)
                    sp.dma_start(w_split[n][:, half_of], w_first[n][half_of].bitcast(F32)).then_inc(w_kept[n], 16)

            def store_y(b, t, index):
                wait_apart(sp, side_retired, index + 1)
                sp.dma_start(out[b, t * P:(t + 1) * P, :], xbuf[:, t % 4, :]).then_inc(y_stored[t % 4], 16)

            sp.dma_start(ident[:, :], ident_in).then_inc(const_loaded, 16)
            for t in range(4):
                load_x(0, t, False)
            for n in FIRST_ORDER:
                w = {"q": wq, "k": wk, "v": wv}[n]
                sp.dma_start(w_whole[n], w.rearrange("(c p) o -> p c o", p=P)).then_inc(w_arrived[n], 16)
            sp.dma_start(pick_whole, pick_in).then_inc(pick_loaded, 16)
            for t in range(4, T):
                wait(sp, side_computed, HEAD.index(("hT", t - 4)) + 1)
                load_x(0, t, False)
            keep_w("k")
            keep_w("q")
            load_adj(0, 0)
            stack_k(0, 0, HEAD.index(("k", 0)))
            stack_k(0, 1, HEAD.index(("k", 1)), first_part["k", 1])
            wait(sp, side_computed, HEAD.index(("q", 1)) + 1)
            wait(sp, w_kept["q"], 32)
            stack_q(0, HEAD.index(("q", 0)), 0, first_part["q", 0])
            load_adj(0, 1)
            load_adj(0, 2)
            wait(sp, w_kept["k"], 32)
            load_w(1, "k")
            stack_q(1, HEAD.index(("q", 1)), 0)
            keep_w("v")
            load_adj(0, 3)
            wait(sp, w_kept["v"], 32)
            load_w(1, "v")
            for t in range(4, T):
                load_adj(0, t)
            sp.dma_start(wo_sb[:, :, :], wo.rearrange("(c p) o -> p c o", p=P)).then_inc(wo_loaded, 16)
            wait(sp, side_computed, HEAD.index(("vT", 1)) + 1)

            def body(b, first, last):
                for tick in range(BSLOTS):
                    g, group_tick = tick // SLOTS, tick % SLOTS
                    for gu, u in units_ending(tick - 1, first, last):
                        index = unit_index(b, first, last, gu, u)
                        bf, gf = fed(b, gu, u)
                        if u in (("k", 1), ("q", 1), ("vT", 1)):
                            nb, ng, nn = bf, gf, {"k": "q", "vT": "k", "q": "v"}[u[0]]
                            if u[0] != "k":
                                nb, ng = (bf, gf + 1) if gf + 1 < G else (bf + 1, 0)
                            if not (last and (ng == 0)):
                                wait_apart(sp, side_computed, index + 1)
                                load_w(ng, nn)
                        if u[0] == "k":
                            stack_k((gu + 1) % 2, u[1], index)
                        if u[0] == "q":
                            stack_q(u[1], index, b * STEPS + gu * T * J + (T * J // 2 if u[1] == 0 else 0))
                        if u[0] == "o":
                            store_y(b - 1, u[1], index)
                            if u[1] < 4:
                                load_x(b - 1, u[1] + 4, True)
                        if u[0] == "hT" and u[1] < 4:
                            wait_apart(sp, side_computed, index + 1)
                            load_x(b + 1, u[1] + 4, False)
                    if g == G - 1 and not last and group_tick % 8 == 7:
                        t = group_tick // 8
                        wait_apart(sp, max_done, b * STEPS + (g * T + t) * J + J)
                        load_adj(b + 1, t)
                    if g == 1 and group_tick in (10, 12, 14, 16) and not last:
                        t = (group_tick - 10) // 2
                        if not first:
                            wait_apart(sp, y_stored[t], b * 2 * 16)
                        load_x(b + 1, t, False)
                    if g == G - 1 and group_tick in (52, 54, 56, 58):
                        t = (group_tick - 52) // 2
                        if last:
                            wait_apart(sp, y_stored[t], b * 2 * 16)
                        else:
                            wait_apart(sp, side_computed, unit_index(b, first, last, g, ("hT", t + 4)) + 1)
                        load_x(b, t, True)

            def tail():
                for t in range(T):
                    store_y(B - 1, t, end_index(("o", t)))
                    if t < 4:
                        load_x(B - 1, t + 4, True)
                for i in range(4):
                    wait_apart(sp, y_stored[i], B * 2 * 16)

            bodies(sp, body, tail)

        @block.tensor
        def _(pe):
            def side_part(b, g, unit, p, end, index, head=False, bank=side[:, :], behind=0):
                kind, c = unit
                if p == 0:
                    wait(pe, side_retired, index - behind)
                if kind == "hT":
                    wait(pe, normed, b * T + c + 1)
                    for i in range(KC):
                        last = nc.tensor.transpose(bank[:, i * P:(i + 1) * P],
                                                   xbuf[:, c % 4, i * P:(i + 1) * P], ident[:, :])
                elif kind in ("k", "q", "vT"):
                    n = kind[0]
                    slot = w_slot(g, n)
                    if head:
                        if p == 0:
                            wait(pe, w_hi_set, FIRST_ORDER.index(n) + 1)
                            wait(pe, w_lo_set, FIRST_ORDER.index(n) + 1)
                        weights = [w_first[n][w][:, p, 0:P] for w in range(2)]
                    else:
                        if p == 0 and unit != ("q", 1):
                            wait(pe, w_loaded[slot], w_count(b, g, n))
                        weights = [w_part[:, slot, w, p, :] for w in range(2)]
                    for i, (w, h) in enumerate(((0, hT_hi), (0, hT_lo), (1, hT_hi))):
                        last = nc.tensor.matmul(bank[:, :], weights[w], h[:, p, c * D:(c + 1) * D],
                                                start=p == 0 and i == 0, stop=p == KC - 1 and i == 2)
                elif kind == "v":
                    for i in range(4):
                        last = nc.tensor.transpose(bank[:, i * P:(i + 1) * P], v_sb[:, g % 2, c * 4 + i, :],
                                                   ident[:, :])
                elif kind == "rT":
                    wait(pe, r_ready, b * G * 2 + g * 2 + c + 1)
                    last = nc.tensor.transpose(bank[0:32, 0:P], rinv_parts[:, :].bitcast(F32), ident[:, :])
                elif kind == "rB":
                    for i in range(4):
                        last = nc.tensor.matmul(bank[:, i * P:(i + 1) * P], pick[:, i, :], rT[:, :],
                                                start=True, stop=True)
                elif kind == "o":
                    if p == 0 and c == 0:
                        wait(pe, wo_loaded, 16)
                    last = nc.tensor.matmul(bank[:, :], oT[:, p, c * P:(c + 1) * P], wo_sb[:, p, :],
                                            start=p == 0, stop=p == KC - 1)
                if end:
                    last.then_inc(side_computed, 1)

            def transposes(tile, t, mi):
                if mi == 0:
                    wait(pe, exp_done, tile * J + J)
                if mi >= 2:
                    brought(pe, tile, mi - 2)
                else:
                    brought(pe, tile - 1, mi + 6)
                for j in range(J):
                    last = nc.tensor.transpose(blockT[:, mi % 2, j * P:(j + 1) * P],
                                               probs[:, t % 2, j, mi * P:(mi + 1) * P], ident[:, :])
                last.then_inc(block_done, 1)

            def products(tile, half_index, gi, t, mi):
                brought(pe, tile, mi)
                if mi == 0 and t % 4 == 0:
                    wait(pe, o_brought, half_index)
                for j in range(J):
                    last = nc.tensor.matmul(o_acc[j * HD:(j + 1) * HD, (t % 4) * P:(t % 4 + 1) * P],
                                            v_sb[:, gi % 2, mi, j * HD:(j + 1) * HD],
                                            probsT[:, mi % 4, j * P:(j + 1) * P],
                                            start=mi == 0, stop=mi == 7, tile_position=(0, j * HD))
                last.then_inc(pv_done, 1)

            wait(pe, const_loaded, 16)
            for n, unit in enumerate(HEAD):
                for p in range(1 if unit[0] in ("hT", "v") else 4):
                    side_part(0, 0, unit, p, unit[0] in ("hT", "v") or p == 3, n, head=True, bank=head_bank(n),
                              behind=3 if unit[0] in ("hT", "q") else 0)

            def body(b, first, last):
                for tick in range(BSLOTS + (TAIL if last else 0)):
                    g, t, mi = tick // SLOTS, tick % SLOTS // 8, tick % 8
                    if tick < BSLOTS and mi % 2 == 0:
                        j = mi // 2
                        s = tick // 2
                        if t == 0:
                            for c in range(2):
                                wait(pe, k_stacked[c][j], (b * G + g + 1) * 16 * 4)
                        if t % 4 == 0:
                            wait(pe, q_stacked[t // 4][j], (b * G + g + 1) * 16 * 4)
                        wait(pe, exp_done, b * STEPS + s - 1)
                        for c in range(2):
                            mm = nc.tensor.matmul(scores[:, s % 2, c * D:(c + 1) * D],
                                                  q_stack[:, j, t * P:(t + 1) * P],
                                                  k_stack[:, g % 2, j, c * D:(c + 1) * D], start=True, stop=True)
                        mm.then_inc(qk_done, 1)
                    i = tick - T_LAG
                    if not (first and i < 0) and i < BSLOTS:
                        transposes(b * G * T + i // 8, i // 8 % T, i % 8)
                    for s, gu, u, p, end in PLAN:
                        if s != tick or not exists(gu, u, first, last):
                            continue
                        if u[0] == "hT":
                            bb, gg = b + 1, 0
                        elif u[0] in ("k", "q", "vT", "v"):
                            bb, gg = fed(b, gu, u)
                        elif u in (("rT", 1), ("rB", 1)):
                            bb, gg = b, gu - 1
                        else:
                            bb, gg = b, gu
                        side_part(bb, gg, u, p, end, unit_index(b, first, last, gu, u))
                    if tick % 2 == PV_LAG % 2:
                        continue
                    for i in (tick - PV_LAG - 1, tick - PV_LAG):
                        if not (first and i < 0) and i < BSLOTS:
                            products(b * G * T + i // 8, b * G * 2 + i // 32, i // SLOTS % G, i // 8 % T, i % 8)

            def tail():
                for unit in END:
                    behind = unit[1] % 4 if unit[0] == "o" else 4 if unit == ("rT", 1) else 0
                    for p in range(4 if unit[0] == "o" else 1):
                        side_part(B - 1, G - 1, unit, p, unit[0] != "o" or p == 3, end_index(unit),
                                  bank=end_bank(unit), behind=behind)

            wait(pe, pick_set, 1)
            bodies(pe, body, tail)

        @block.scalar
        def _(act):
            def retire(b, g, unit, index, hi=part[0], head=False, bank=side[:, :]):
                kind, c = unit
                if kind == "hT":
                    act.wait_ge(side_computed, index + 1)
                    nc.scalar.activation(hT_hi[:, :, c * P:(c + 1) * P],
                                         bank[:, :].rearrange("p (i n) -> p i n", i=KC), ACT.Relu
                                         ).then_inc(hi_split, 1)
                elif kind == "vT":
                    act.wait_ge(side_computed, index + 1)
                    nc.scalar.activation(v_sb[:, g % 2, c * 4:(c + 1) * 4, :],
                                         bank[:, :].rearrange("p (i n) -> p i n", i=4), ACT.Copy
                                         ).then_inc(side_retired, 1)
                elif kind == "v":
                    act.wait_ge(side_computed, index + 1)
                    nc.scalar.activation(v_sb[:, g % 2, c * 4:(c + 1) * 4, :],
                                         bank[:, :].rearrange("p (i n) -> p i n", i=4), ACT.Copy
                                         ).then_inc(side_retired, 1)
                elif kind == "k":
                    act.wait_ge(side_computed, index + 1)
                    if head:
                        wait(act, w_lo_set, c)
                    elif c == 0:
                        stacked(q_stacked[1], b * G + g)
                    else:
                        stacked(k_stacked[0], b * G + g + 1)
                    nc.scalar.activation(hi, bank[:, :], ACT.Copy).then_inc(hi_split, 1)
                elif kind == "q":
                    act.wait_ge(side_computed, index + 1)
                    if head:
                        if c == 0:
                            wait(act, w_lo_set, 1)
                        else:
                            stacked(k_stacked[0], 1)
                    else:
                        stacked(k_stacked[1] if c == 0 else q_stacked[0], b * G + g + 1)
                    nc.scalar.activation(hi, bank[:, :], ACT.Copy, scale=SCALE / 2).then_inc(hi_split, 1)

            def stacked(parts, count):
                for j in range(J):
                    wait(act, parts[j], count * 16 * 4)

            def bring(tile, mi):
                act.wait_ge(block_done, tile * 8 + mi + 1)
                wait(act, pv_done, tile * 8 + mi - 3)
                nc.scalar.activation(probsT[:, mi % 4, :], blockT[:, mi % 2, :], ACT.Copy).then_inc(act_brought, 1)

            def bring_o(half_index, pv_count, o_used):
                act.wait_ge(pv_done, pv_count)
                wait(act, side_computed, o_used)
                nc.scalar.activation(oT[:, half_index // 2 % G, half_index % 2 * D:(half_index % 2 + 1) * D],
                                     o_acc[:, :], ACT.Copy).then_inc(o_brought, 1)

            def split_w(n):
                wait(act, w_arrived[n], 16)
                if n == "v":
                    wait(act, w_kept["k"], 32)
                nc.scalar.activation(w_first[n][0], w_whole[n], ACT.Copy).then_inc(w_hi_set, 1)

            for n, unit in enumerate(HEAD):
                if n in SPLIT_AT:
                    split_w(SPLIT_AT[n])
                retire(0, 0, unit, n, first_part.get(unit, part)[0], head=True, bank=head_bank(n))

            def body(b, first, last):
                for tick in range(BSLOTS + (TAIL if last else 0)):
                    g, t, mi = tick // SLOTS, tick % SLOTS // 8, tick % 8
                    i = tick - T_LAG
                    if i % 8 not in DVE_BLOCKS and not (first and i < 0) and i < BSLOTS:
                        bring(b * G * T + i // 8, i % 8)
                    if tick < BSLOTS and mi % 2 == 1:
                        j, s = mi // 2, tick // 2
                        act.wait_ge(max_done, b * STEPS + s + 1)
                        if j == 0:
                            wait(act, block_done, (b * G * T + g * T + t - 1) * 8)
                        nc.scalar.activation(probs[:, t % 2, j, :], scores[:, s % 2, :], ACT.Exp,
                                             bias=neg_max[:, g % 2, t * J + j:t * J + j + 1], scale=-1.0,
                                             accum_out=row_sum[:, g % 2, t * J + j:t * J + j + 1]
                                             ).then_inc(exp_done, 1)
                    i = tick - PV_LAG
                    if i % 32 == 31 and not (first and i < 0) and i < BSLOTS:
                        hh = i // 32
                        o_used = 0
                        if hh in (0, 1) and not first:
                            o_used = unit_index(b, first, last, 0, ("o", 4 * hh + 3)) + 1
                        bring_o(hh, (b * BSLOTS) + i + 1, o_used)
                    for gu, u in units_ending(tick, first, last):
                        bb, gg = fed(b, gu, u) if u[0] in ("k", "q", "vT", "v") else (b, gu)
                        retire(bb, gg, u, unit_index(b, first, last, gu, u))

            bodies(act, body, lambda: None)

        @block.vector
        def _(dve):
            def norm_stats(b, t):
                slot = t % 4
                wait_apart(dve, moments_done, b * T + t)
                dve.wait_ge(x_loaded[slot], norm_loads(b, t))
                nc.vector.bn_stats(stats[:, :], xbuf[:, slot, :]).then_inc(stats_done, 1)

            def norm_moments(b, t):
                slot = t % 4
                wait_apart(dve, stats_done, b * T + t + 1)
                nc.vector.bn_aggr(moments[:, slot, :], stats[:, :]).then_inc(moments_done, 1)

            def norm_loads(b, t):
                before = 0 if isinstance(b, int) and b == 0 else 4 * b - 2
                return (before + t // 4 + 1) * 16

            def normalise(b, t):
                slot = t % 4
                dve.wait_ge(rstd_done, b * T + t + 1)
                nc.vector.tensor_scalar(xbuf[:, slot, :], xbuf[:, slot, :], moments[:, slot, 0:1],
                                        rstd[:, slot:slot + 1], ALU.subtract, ALU.mult).then_inc(normed, 1)

            def retire(b, g, unit, index, split=0, parts=part, bank=side[:, :]):
                kind, c = unit
                if kind in ("k", "q"):
                    dve.wait_ge(hi_split, split + 1)
                    nc.vector.scalar_tensor_tensor(parts[1], bank[:, :], 1.0 if kind == "k" else SCALE / 2,
                                                   parts[0].bitcast(F32), ALU.mult, ALU.subtract
                                                   ).then_inc(side_retired, 1)
                elif kind == "hT":
                    dve.wait_ge(hi_split, split + 1)
                    nc.vector.scalar_tensor_tensor(hT_lo[:, :, c * P:(c + 1) * P],
                                                   bank[:, :].rearrange("p (i n) -> p i n", i=KC), 0.0,
                                                   hT_hi[:, :, c * P:(c + 1) * P].bitcast(F32),
                                                   ALU.max, ALU.subtract).then_inc(side_retired, 1)
                elif kind == "rT":
                    dve.wait_ge(side_computed, index + 1)
                    nc.vector.tensor_copy(rT[:, :], bank[0:32, 0:P]).then_inc(side_retired, 1)
                elif kind == "rB":
                    dve.wait_ge(side_computed, index + 1)
                    dve.wait_ge(o_brought, (b * G + g) * 2 + c + 1)
                    o_half = oT[:, g % G, c * D:(c + 1) * D]
                    nc.vector.tensor_tensor(o_half, bank[:, :], o_half, ALU.mult).then_inc(side_retired, 1)
                elif kind == "o":
                    dve.wait_ge(side_computed, index + 1)
                    dve.wait_ge(x_loaded[c % 4], sum_loads(b, c))
                    nc.vector.tensor_tensor(xbuf[:, c % 4, :], bank[:, :], xbuf[:, c % 4, :],
                                            ALU.add).then_inc(side_retired, 1)

            def sum_loads(b, t):
                if isinstance(b, int) and b == B - 1:
                    return (b * 4 + 2 + t // 4 + 1) * 16
                return (b * 4 + 4 + t // 4 + 1) * 16

            def invert(b, g, c, transposed, step):
                half_index = (b * G + g) * 2 + c
                cols = slice(16 * c, 16 * c + 16)
                rinv_hi = rinv_parts[:, 0:16]
                rinv_lo = rinv_parts[:, 16:32]
                rinv = rinv_lo.bitcast(F32)
                if step > 0:
                    dve.wait_ge(r_step, half_index * 5 + 1 + step)
                if step == 0:
                    dve.wait_ge(exp_done, (b * G + g) * T * J + 16 * (c + 1))
                    wait(dve, side_computed, transposed)
                    nc.vector.reciprocal(rinv, row_sum[:, g % 2, cols]).then_inc(r_step, 1)
                    nc.vector.tensor_scalar(keep[:, :], neg_max[:, g % 2, cols], 0.0, None,
                                            ALU.not_equal).then_inc(r_step, 1)
                if step == 1:
                    nc.vector.scalar_tensor_tensor(keep[:, :], row_sum[:, g % 2, cols], float(N), keep[:, :],
                                                   ALU.is_lt, ALU.max).then_inc(r_step, 1)
                if step == 2:
                    nc.vector.tensor_tensor(rinv, rinv, keep[:, :], ALU.mult).then_inc(r_step, 1)
                if step == 3:
                    nc.vector.tensor_copy(rinv_hi, rinv).then_inc(r_step, 1)
                if step == 4:
                    nc.vector.tensor_tensor(rinv_lo, rinv, rinv_hi.bitcast(F32), ALU.subtract).then_inc(r_ready, 1)

            nc.vector.memset(half[:, :], -0.5).then_inc(half_set, 1)

            def split_w(n):
                dve.wait_ge(w_hi_set, FIRST_ORDER.index(n) + 1)
                nc.vector.tensor_tensor(w_first[n][1], w_whole[n], w_first[n][0].bitcast(F32), ALU.subtract
                                        ).then_inc(w_lo_set, 1)

            def retire_head(n):
                unit = HEAD[n]
                retire(0, 0, unit, n, sum(u[0] in SPLIT for u in HEAD[:n]), first_part.get(unit, part), head_bank(n))

            norm_stats(0, 0)
            norm_moments(0, 0)
            for t in range(4):
                if t < 3:
                    norm_stats(0, t + 1)
                    norm_moments(0, t + 1)
                normalise(0, t)
            retire_head(0)
            retire_head(1)
            split_w("k")
            retire_head(2)
            retire_head(3)
            split_w("q")
            for t in range(4, T):
                norm_stats(0, t)
                norm_moments(0, t)
                if t > 4:
                    normalise(0, t - 1)
                if t == 6:
                    retire_head(4)
            normalise(0, T - 1)
            for n in range(5, 9):
                retire_head(n)
            dve.wait_ge(pick_loaded, 16)
            nc.vector.tensor_copy(pick[:, :, :], pick_whole).then_inc(pick_set, 1)
            for n in range(9, HEAD_UNITS):
                if n in SPLIT_AT:
                    split_w(SPLIT_AT[n])
                retire_head(n)

            def body(b, first, last):
                for tick in range(BSLOTS + (TAIL if last else 0)):
                    g, t, mi = tick // SLOTS, tick % SLOTS // 8, tick % 8
                    group_tick = tick % SLOTS
                    if tick < BSLOTS and mi % 2 == 0:
                        j, s = mi // 2, tick // 2
                        wait_apart(dve, qk_done, b * STEPS + s + 1)
                        if g == 0 and j == 0:
                            wait_apart(dve, adj_loaded[t], (b + 1) * 16)
                        nc.vector.tensor_tensor_reduce(
                            out=scores[:, s % 2, :], in0=scores[:, s % 2, :], in1=adj_sb[:, t, :], scale=-2.0,
                            scalar=BIG, op0=ALU.add, op1=ALU.min,
                            accum_out=neg_max[:, g % 2, t * J + j:t * J + j + 1]).then_inc(max_done, 1)
                    i = tick - T_LAG
                    if i % 8 in DVE_BLOCKS and not (first and i < 0) and i < BSLOTS:
                        tile, m = b * G * T + i // 8, i % 8
                        dve.wait_ge(block_done, tile * 8 + m + 1)
                        wait(dve, pv_done, tile * 8 + m - 3)
                        nc.vector.tensor_copy(probsT[:, m % 4, :], blockT[:, m % 2, :]).then_inc(dve_brought, 1)
                    for s, gu, u, _, _ in PLAN:
                        step = tick - (s - INVERT_STEPS - 1)
                        if u[0] == "rT" and 0 <= step < INVERT_STEPS and exists(gu, u, first, last):
                            gg = gu - 1 if u[1] == 1 else gu
                            invert(b, gg, u[1], rt_last(b, first, last, gu, u), step)
                    step = tick - (BSLOTS + 7)
                    if last and 0 <= step < INVERT_STEPS:
                        invert(b, G - 1, 1, unit_index(b, first, last, G - 1, ("rT", 0)) + 1, step)
                    if not last:
                        for t2, slots in enumerate(NORM_AT):
                            for step, s in zip((norm_stats, norm_moments, normalise), slots):
                                if s == tick:
                                    step(b + 1, t2)
                    for gu, u in units_ending(tick, first, last):
                        bb, gg = (b, gu)
                        if u[0] in ("k", "q", "vT", "v"):
                            bb, gg = fed(b, gu, u)
                        elif u[0] == "hT":
                            bb = b + 1
                        elif u[0] == "rB" and u[1] == 1:
                            bb, gg = (b, gu - 1) if gu > 0 else (b - 1, G - 1)
                        elif u[0] == "o":
                            bb = b - 1
                        retire(bb, gg, u, unit_index(b, first, last, gu, u),
                               split_index(b, gu, u) if u[0] in SPLIT else 0)

            def rt_last(b, first, last, gu, u):
                if u == ("rT", 0):
                    if first and gu == 0:
                        return 0
                    return unit_index(b, first, last, gu, ("rT", 1)) + 1
                if gu > 0:
                    return unit_index(b, first, last, gu - 1, ("rT", 0)) + 1
                return b * UNITS + (HEAD_UNITS - LACK) - (UNITS - RANK[False, False][G - 1, ("rT", 0)]) + 1

            def tail():
                for unit in END:
                    retire(B - 1, G - 1, unit, end_index(unit), bank=end_bank(unit))

            bodies(dve, body, tail)

        @block.gpsimd
        def _(pool):
            pool.wait_ge(half_set, 1)
            with pool.Fori(0, B) as b:
                for t in range(T):
                    slot = t % 4
                    wait_apart(pool, moments_done, b * T + t + 1)
                    nc.gpsimd.tensor_scalar(var_eps[:, slot:slot + 1], moments[:, slot, 1:2], EPS, None,
                                            ALU.add).then_inc(eps_added, 1)
                    pool.wait_ge(eps_added, b * T + t + 1)
                    nc.gpsimd.tensor_tensor(rstd[:, slot:slot + 1], var_eps[:, slot:slot + 1], half[:, :],
                                            ALU.pow).then_inc(rstd_done, 1)


def kernel(x, adj, L0_gnn_Wq, L0_gnn_Wk, L0_gnn_Wv, L0_gnn_Wo):
    import numpy as np
    import concourse.bacc as bacc
    from concourse.bass_utils import run_bass_kernel_spmd

    pick = np.zeros((2, 4, J, 4, J, HD), np.float32)
    for t in range(4):
        for j in range(J):
            pick[:, t, j, t, j] = 1
    arrays = {
        "x": np.ascontiguousarray(x), "adj": np.ascontiguousarray(adj),
        "wqT": np.ascontiguousarray(np.transpose(L0_gnn_Wq)), "wkT": np.ascontiguousarray(np.transpose(L0_gnn_Wk)),
        "wvT": np.ascontiguousarray(np.transpose(L0_gnn_Wv)), "woT": np.ascontiguousarray(np.transpose(L0_gnn_Wo)),
        "ident": np.eye(P, dtype=np.float32), "pick": pick.reshape(2 * 4 * J, 4, P),
    }
    arrays = {f"in_{n}": a for n, a in arrays.items()}
    nc = bacc.Bacc("TRN2", target_bir_lowering=False, num_devices=1)
    aps = [nc.dram_tensor(n, a.shape, mybir.dt.from_np(a.dtype), kind="ExternalInput").ap() for n, a in arrays.items()]
    out = nc.dram_tensor("out", (B, N, D), F32, kind="ExternalOutput").ap()
    adj_gnn(nc, *aps, out)
    r = run_bass_kernel_spmd(nc, [arrays], core_ids=[0])
    return r.results[0]["out"]
```
